# Optimizing a Trainium2 kernel written in Bass

```python
import numpy as np
import jax
import jax.numpy as jnp

def _softmax(x, axis=-1):
    return jax.nn.softmax(x, axis=axis)

def _gelu(x):
    return jax.nn.gelu(x, approximate=True)

def _silu(x):
    return jax.nn.silu(x)

def _sigmoid(x):
    return jax.nn.sigmoid(x)

def _layernorm(x, axis=-1, eps=1e-05):
    m = jnp.mean(x, axis=axis, keepdims=True)
    v = jnp.var(x, axis=axis, keepdims=True)
    return (x - m) / jnp.sqrt(v + eps)

def _scatter_add(tgt, idx, src, axis=0):
    return tgt.at[idx].add(src)

def _segment_sum(src, seg, n):
    return jax.ops.segment_sum(src, seg, n)
kernel_name = 'mk_seq_preln_d1_jaxref_r8_2ebc8a'

def setup_inputs(seed: int=0):
    np.random.seed(seed)
    _w = jnp.asarray

    def _L0_attn_setup():
        import jax, jax.numpy as jnp
        import numpy as np
        HIDDEN = 256
        N_HEADS = 16
        HEAD_DIM = HIDDEN // N_HEADS

        def rotate_half(x):
            x1, x2 = jnp.split(x, 2, axis=-1)
            return jnp.concatenate([-x2, x1], axis=-1)
        key = jax.random.key(seed)
        k0, k1, k2, k3, k4 = jax.random.split(key, 5)
        B, S = (1, 256)
        scale = 1.0 / np.sqrt(HIDDEN)
        return {'hidden_states': jax.random.normal(k0, (B, S, HIDDEN), dtype=jnp.float32), 'Wq': jax.random.normal(k1, (HIDDEN, HIDDEN), dtype=jnp.float32) * scale, 'Wk': jax.random.normal(k2, (HIDDEN, HIDDEN), dtype=jnp.float32) * scale, 'Wv': jax.random.normal(k3, (HIDDEN, HIDDEN), dtype=jnp.float32) * scale, 'Wo': jax.random.normal(k4, (HIDDEN, HIDDEN), dtype=jnp.float32) * scale, 'gate': jnp.zeros((1, N_HEADS, 1, 1), dtype=jnp.float32)}
    _L0_attn_in = _L0_attn_setup()

    def _L0_ffn_setup():
        import jax, jax.numpy as jnp
        import numpy as np
        B, S, D, H = (4, 256, 256, 1024)

        def fwht(x):
            orig_shape = x.shape
            n = orig_shape[-1]
            x = x.reshape(-1, n)
            h = 1
            while h < n:
                xb = x.reshape(-1, n // (2 * h), 2, h)
                a = xb[:, :, 0, :]
                b = xb[:, :, 1, :]
                x = jnp.stack([a + b, a - b], axis=2).reshape(-1, n)
                h *= 2
            scale = jnp.asarray(1.0 / np.sqrt(n), dtype=x.dtype)
            return (x * scale).reshape(orig_shape)
        key = jax.random.key(seed)
        kx, k1, k2, k3 = jax.random.split(key, 4)
        x = jax.random.normal(kx, (B, S, D), dtype=jnp.float32)
        W1 = jax.random.normal(k1, (H, D), dtype=jnp.float32) * (1.0 / np.sqrt(D))
        W2 = jax.random.normal(k2, (D, H), dtype=jnp.float32) * (1.0 / np.sqrt(H))
        W3 = jax.random.normal(k3, (H, D), dtype=jnp.float32) * (1.0 / np.sqrt(D))
        return {'x': x, 'W1': W1, 'W2': W2, 'W3': W3}
    _L0_ffn_in = _L0_ffn_setup()
    _d = {'L0_attn_hidden_states': _L0_attn_in['hidden_states'], 'L0_attn_Wq': _L0_attn_in['Wq'], 'L0_attn_Wk': _L0_attn_in['Wk'], 'L0_attn_Wv': _L0_attn_in['Wv'], 'L0_attn_Wo': _L0_attn_in['Wo'], 'L0_attn_gate': _L0_attn_in['gate'], 'L0_ffn_W1': _L0_ffn_in['W1'], 'L0_ffn_W2': _L0_ffn_in['W2'], 'L0_ffn_W3': _L0_ffn_in['W3']}
    _x0 = _d['L0_attn_hidden_states']
    _d['L0_attn_hidden_states'] = jax.random.normal(jax.random.fold_in(jax.random.key(seed), 1), (4, 256, 256), dtype=_x0.dtype)
    del _x0
    return _d

def reference(L0_attn_hidden_states, L0_attn_Wq, L0_attn_Wk, L0_attn_Wv, L0_attn_Wo, L0_attn_gate, L0_ffn_W1, L0_ffn_W2, L0_ffn_W3):

    def _L0_attn_ref(hidden_states, Wq, Wk, Wv, Wo, gate):
        import jax, jax.numpy as jnp
        import numpy as np
        HIDDEN = 256
        N_HEADS = 16
        HEAD_DIM = HIDDEN // N_HEADS

        def rotate_half(x):
            x1, x2 = jnp.split(x, 2, axis=-1)
            return jnp.concatenate([-x2, x1], axis=-1)
        B, S, H = hidden_states.shape
        q = hidden_states @ Wq.T
        k = hidden_states @ Wk.T
        v = hidden_states @ Wv.T
        inv_freq = 1.0 / 10000.0 ** (jnp.arange(0, H, 2, dtype=jnp.float32) / H)
        t = jnp.arange(S, dtype=jnp.float32)
        freqs = t[:, None] * inv_freq[None, :]
        emb = jnp.concatenate([freqs, freqs], axis=-1)[None]
        cos, sin = (jnp.cos(emb), jnp.sin(emb))
        q = q * cos + rotate_half(q) * sin
        k = k * cos + rotate_half(k) * sin

        def split_heads(x):
            return x.reshape(B, S, N_HEADS, HEAD_DIM).transpose(0, 2, 1, 3)
        q, k, v = (split_heads(q), split_heads(k), split_heads(v))
        k_feat = jax.nn.elu(k) + 1.0
        memory = jnp.einsum('bhsd,bhse->bhde', k_feat, v)
        norm_term = k_feat.sum(axis=2)
        q_feat = jax.nn.elu(q) + 1.0
        mem_out = jnp.einsum('bhsd,bhde->bhse', q_feat, memory)
        denom = jnp.einsum('bhsd,bhd->bhs', q_feat, norm_term)[..., None]
        mem_out = mem_out / denom
        scale = 1.0 / jnp.sqrt(jnp.float32(HEAD_DIM))
        scores = jnp.einsum('bhqd,bhkd->bhqk', q, k) * scale
        attn = jnp.einsum('bhqk,bhkd->bhqd', jax.nn.softmax(scores, axis=-1), v)
        g = jax.nn.sigmoid(gate)
        combined = g * mem_out + (1.0 - g) * attn
        combined = combined.transpose(0, 2, 1, 3).reshape(B, S, H)
        return combined @ Wo.T

    def _L0_ffn_ref(x, W1, W2, W3):
        import jax, jax.numpy as jnp
        import numpy as np
        B, S, D, H = (4, 256, 256, 1024)

        def fwht(x):
            orig_shape = x.shape
            n = orig_shape[-1]
            x = x.reshape(-1, n)
            h = 1
            while h < n:
                xb = x.reshape(-1, n // (2 * h), 2, h)
                a = xb[:, :, 0, :]
                b = xb[:, :, 1, :]
                x = jnp.stack([a + b, a - b], axis=2).reshape(-1, n)
                h *= 2
            scale = jnp.asarray(1.0 / np.sqrt(n), dtype=x.dtype)
            return (x * scale).reshape(orig_shape)
        up_gate = jnp.einsum('bsd,hd->bsh', x, W1)
        up_lin = jnp.einsum('bsd,hd->bsh', x, W3)
        hidden = jax.nn.silu(up_gate) * up_lin
        hidden = fwht(hidden)
        out = jnp.einsum('bsh,dh->bsd', hidden, W2)
        return out
    x = L0_attn_hidden_states
    x = x + _L0_attn_ref(_layernorm(x, axis=-1), L0_attn_Wq, L0_attn_Wk, L0_attn_Wv, L0_attn_Wo, L0_attn_gate)
    x = x + _L0_ffn_ref(_layernorm(x, axis=-1), L0_ffn_W1, L0_ffn_W2, L0_ffn_W3)
    return x

_drawn_inputs = setup_inputs


def setup_inputs(seed=0):
    import zlib

    import numpy as np

    out = dict(_drawn_inputs(seed))
    spreads = {'L0_attn_gate': (0.0, 2.0)}
    factors = {}
    for name, (base, spread) in spreads.items():
        noise = np.random.default_rng([zlib.crc32(name.encode()), seed]).standard_normal(out[name].shape)
        drawn = base * np.exp(spread * noise) if base else spread * noise
        out[name] = jnp.asarray(drawn.astype(out[name].dtype))
    for name, factor in factors.items():
        out[name] = (out[name] * factor).astype(out[name].dtype)
    return out
```

```python
from contextlib import ExitStack

import numpy as np

import concourse.bass as bass
from concourse import mybir

F32 = mybir.dt.float32
F32R = mybir.dt.float32r
ALU = mybir.AluOpType
ACT = mybir.ActivationFunctionType
AX = mybir.AxisListType

P = 128
NB, S, D = 4, 256, 256
NH, HD = 16, 16
FF = 1024
TT = S // P
DC = D // P
FC = FF // P
NG = NH // 4
HH = NH // DC
STRIP = 32
VW = HD + 1
MAXROW = 64
EPS = 1e-5
SCALE = HD ** -0.5
C_ID, C_HAD, C_COS, C_SIN, C_MASK = 0, P, 2 * P, 2 * P + S, 2 * P + 2 * S
NCONST = C_MASK + HH


def shape_constants():
    i = np.arange(P)
    bits = i[:, None] & i[None, :]
    parity = np.zeros_like(bits)
    for s in range(7):
        parity ^= (bits >> s) & 1
    inv_freq = (1.0 / np.float32(10000.0) ** (np.arange(0, D, 2, dtype=np.float32) / np.float32(D))).astype(np.float32)
    angle = inv_freq[:, None] * np.arange(S, dtype=np.float32)[None, :]
    c = np.zeros((P, NCONST), np.float32)
    c[:, C_ID:C_ID + P] = np.eye(P)
    c[:, C_HAD:C_HAD + P] = 1 - 2 * parity
    c[:, C_COS:C_COS + S] = np.cos(angle)
    c[:, C_SIN:C_SIN + S] = np.sin(angle)
    c[:, C_MASK:C_MASK + HH] = (i[:, None] // HD == np.arange(HH)[None, :])
    return c


def build(nc, x, wqT, wkT, wvT, woT, gate, w1T, w3T, w2T, const, out):
    with ExitStack() as ctx:
        def sb(name, shape, dt=F32):
            return ctx.enter_context(nc.sbuf_tensor(name, shape, dt))

        def sem(name):
            return ctx.enter_context(nc.semaphore(name))

        def bank(name):
            return ctx.enter_context(nc.psum_tensor(name, [P, 2, 256], F32))

        score_bank = [bank("score_bank0"), bank("score_bank1")]
        exp_bank = [bank("exp_bank0"), bank("exp_bank1")]
        pv_bank = bank("pv_bank")
        misc_bank = [bank("misc_bank0"), bank("misc_bank1")]
        down_bank = bank("down_bank")

        xs = sb("xs", [P, NB, TT, D])
        cst = sb("cst", [P, NCONST])
        ident = cst[:, C_ID:C_ID + P]
        had = cst[:, C_HAD:C_HAD + P]
        cos2 = cst[:, C_COS:C_COS + S].unsqueeze(1).broadcast_to([P, 2, S])
        sin2 = cst[:, C_SIN:C_SIN + S].unsqueeze(1).broadcast_to([P, 2, S])
        mask = cst[:, C_MASK:C_MASK + HH].unsqueeze(2).broadcast_to([P, HH, VW])
        wide_raw = sb("wide_raw", [P, 2, DC, FF])
        narrow_raw = sb("narrow_raw", [P, 2048])
        wqkv_raw = narrow_raw[:, 0:3 * DC * D].rearrange("p (m c n) -> p m c n", m=3, c=DC)
        w2_raw = narrow_raw[:, :].rearrange("p (c n) -> p c n", c=FC)
        rden = narrow_raw[:, :].rearrange("p (k n) -> p k n", k=2)
        ffn_work = [wide_raw[:, 0, 0, 256 * k:256 * k + 256] for k in range(3)]
        wqkv_hi = sb("wqkv_hi", [P, 3, DC, D], F32R)
        wqkv_lo = sb("wqkv_lo", [P, 3, DC, D], F32R)
        w13_hi = sb("w13_hi", [P, 2, DC, FF], F32R)
        w13_lo = sb("w13_lo", [P, 2, DC, FF], F32R)
        w2_hi = sb("w2_hi", [P, FC, D], F32R)
        w2_lo = sb("w2_lo", [P, FC, D], F32R)
        wo = sb("wo", [P, NG, D])
        stats = sb("stats", [P, TT, 6])
        mv = sb("mv", [P, TT, 2])
        var_eps = sb("var_eps", [P, TT])
        rstd = sb("rstd", [P, TT])
        mhalf = sb("mhalf", [P, TT])
        xn = sb("xn", [P, TT, D])
        hT_hi = sb("hT_hi", [P, DC, S], F32R)
        hT_lo = sb("hT_lo", [P, DC, S], F32R)
        h2T_hi = sb("h2T_hi", [P, DC, S], F32R)
        h2T_lo = sb("h2T_lo", [P, DC, S], F32R)
        prod = sb("prod", [P, 4, 2, S])
        elu = prod[:, 0:2, :, :]
        roped = sb("roped", [P, DC, 2, S])
        part_hi = sb("part_hi", [P, DC, 2, S], F32R)
        part_lo = sb("part_lo", [P, DC, 2, S], F32R)
        feat = sb("feat", [P, DC, 2, S])
        q_stack = sb("q_stack", [P, NH, S], F32R)
        k_stack = sb("k_stack", [P, NH, S], F32R)
        v_strips = [sb("v_strips0", [P, TT, NH, STRIP]), sb("v_strips1", [P, TT, NH, STRIP])]
        kfT = sb("kfT", [P, TT, D])
        mem = sb("mem", [P, DC, HH, STRIP])
        rowmax = sb("rowmax", [P, TT, NH])
        nmT_hi = sb("nmT_hi", [TT * NH, P], F32R)
        nmT_lo = sb("nmT_lo", [TT * NH, P], F32R)
        prob = sb("prob", [P, 8, TT, S])
        w2_a = prob[:, 0:4, :, :].rearrange("p a b n -> p (a b) n")
        w2_b = prob[:, 4:8, :, :].rearrange("p a b n -> p (a b) n")
        att = sb("att", [P, NG, S])
        lin = wide_raw[:, 0, 1, :].rearrange("p (g n) -> p g n", g=NG)
        den = sb("den", [P, 2, STRIP])
        inv = sb("inv", [P, 2, STRIP])
        ginv = sb("ginv", [P, 2, STRIP])
        ginv_rows = wide_raw[0:4, 1, :, :]
        gcol = sb("gcol", [P, 1])
        gexp = sb("gexp", [P, 1])
        gsum = sb("gsum", [P, 1])
        gate2 = sb("gate2", [P, 2])
        hid_hi = sb("hid_hi", [P, 3, S], F32R)
        hid_lo = sb("hid_lo", [P, 3, S], F32R)
        parts = nc.dram_tensor("parts", [NB, 2, DC, 2, P, S], F32, kind="Internal").ap()

        x_in = [sem(f"x_in{b}") for b in range(NB)]
        (const_in, wqkv_in, w13_in, w2_in, wo_in, gate_in, mhalf_set, wo_zero, stack_zero, k_zero, v_const, mem_zero, wqkv_hi_s, wqkv_lo_s, w13_hi_s, w13_lo_s,
         had_ps, had_sb, fly, w2_hi_s, w2_lo_s, gate_exp, gate_s) = [sem(n) for n in (
             "const_in wqkv_in w13_in w2_in wo_in gate_in mhalf_set wo_zero stack_zero k_zero v_const mem_zero wqkv_hi_s wqkv_lo_s w13_hi_s w13_lo_s "
             "had_ps had_sb fly w2_hi_s w2_lo_s gate_exp gate_s").split()]
        (ln_stats, ln_mv, ln_ve, ln_rstd, ln_xn, hT_ps, hT_hi_s, hT_lo_s, h2T_ps, h2T_hi_s, h2T_lo_s) = [
            sem(n) for n in ("ln_stats ln_mv ln_ve ln_rstd ln_xn hT_ps hT_hi_s hT_lo_s h2T_ps h2T_hi_s h2T_lo_s").split()]
        (qk_ps, v_ps, v_sb, rope_prod, rope_sum, part_hi_s, part_lo_s, parts_out, neg_s, elu_s, feat_s, kfT_ps,
         kfT_sb, mem_ps, mem_sb, lin_ps, lin_sb) = [sem(n) for n in (
             "qk_ps v_ps v_sb rope_prod rope_sum part_hi_s part_lo_s parts_out neg_s elu_s feat_s kfT_ps "
             "kfT_sb mem_ps mem_sb lin_ps lin_sb").split()]
        stack_in = [sem("stack_in0"), sem("stack_in1")]
        (score_ps, rowmax_s, maxT_ps, nm_hi_s, nm_lo_s, maxrow_in, exp_ps, prob_s, pv_group, att_sb, den_in, den_lin_in,
         inv_s, ginv_s, ginv_row, rden_in, norm_att, norm_lin, comb_s, wo_ps, x2_s) = [sem(n) for n in (
             "score_ps rowmax_s maxT_ps nm_hi_s nm_lo_s maxrow_in exp_ps prob_s pv_group att_sb den_in den_lin_in "
             "inv_s ginv_s ginv_row rden_in norm_att norm_lin comb_s wo_ps x2_s").split()]
        (up_ps, tanh_s, gated_s, hid_s, hid_hi_s, hid_lo_s, down_ps, y_s, y_out) = [sem(n) for n in (
            "up_ps tanh_s gated_s hid_s hid_hi_s hid_lo_s down_ps y_s y_out").split()]

        block = ctx.enter_context(nc.Block())
        ROUNDS = range(-1, NB + 1)

        def has(b):
            return 0 <= b < NB

        LN_ORDER = []
        LN_ORDER.append((1, 0))
        for r in ROUNDS:
            if has(r - 1):
                LN_ORDER.append((2, r - 1))
            if has(r + 2):
                LN_ORDER.append((1, r + 2))
        LN = {key: n for n, key in enumerate(LN_ORDER)}

        def xn_read(n):
            which, b = LN_ORDER[n]
            return (hT_ps if which == 1 else h2T_ps), b + 1

        @block.sync
        def _(sp):
            def xv(ap, b):
                return ap[b].rearrange("(t p) d -> p t d", p=P)

            sp.dma_start(xs[:, 0], xv(x, 0)).then_inc(x_in[0], 16)
            for m, w in enumerate((wqT, wkT)):
                sp.dma_start(wqkv_raw[:, m], w.rearrange("(c p) n -> p c n", p=P)).then_inc(wqkv_in, 16)
            for b in range(1, NB):
                sp.dma_start(xs[:, b], xv(x, b)).then_inc(x_in[b], 16)
            for m, w in enumerate((w1T, w3T)):
                sp.dma_start(wide_raw[:, m], w.rearrange("(c p) n -> p c n", p=P)).then_inc(w13_in, 16)

            sp.wait_ge(wqkv_hi_s, 1)
            sp.wait_ge(wqkv_lo_s, 1)
            sp.dma_start(w2_raw, w2T.rearrange("(c p) n -> p c n", p=P)).then_inc(w2_in, 16)

            def write_parts(b):
                sp.wait_ge(part_hi_s, b + 1)
                sp.dma_start(parts[b, 0].rearrange("c m p n -> p c m n"), part_hi[:].bitcast(F32)).then_inc(parts_out, 16)
                sp.wait_ge(part_lo_s, b + 1)
                sp.dma_start(parts[b, 1].rearrange("c m p n -> p c m n"), part_lo[:].bitcast(F32)).then_inc(parts_out, 16)

            def load_stacks(b, c):
                sp.wait_ge(parts_out, 32 * (b + 1))
                if b == 0:
                    sp.wait_ge(stack_zero, 2)
                else:
                    sp.wait_ge(exp_ps, NH * (b - 1) + HH * (c + 1))
                for m, stack, slots in ((0, q_stack, (0, 1, 0)), (1, k_stack, (0, 0, 1))):
                    for s, half in enumerate(slots):
                        sp.dma_start(stack[HD * s:HD * s + HD, HH * c:HH * c + HH, :].bitcast(F32),
                                     parts[b, half, c, m].rearrange("(h d) n -> d h n", d=HD)).then_inc(stack_in[c], 16)

            def load_max(b):
                for k, (t, ready) in enumerate(((nmT_hi, nm_hi_s), (nmT_lo, nm_lo_s))):
                    sp.wait_ge(ready, b + 1)
                    for tt in range(TT):
                        sp.dma_start(q_stack[MAXROW + k:MAXROW + k + 1, :, tt * P:tt * P + P].bitcast(F32),
                                     t[tt * NH:tt * NH + NH, :].bitcast(F32)).then_inc(maxrow_in, 16)

            def den_rows(src, k, signal):
                sp.dma_start(den[:, k, :], src[HD:P:STRIP].rearrange("p g n -> p (g n)")).then_inc(signal, 16)

            for r in ROUNDS:
                if has(r + 1):
                    write_parts(r + 1)
                    if r < 0:
                        load_stacks(0, 0)
                        load_stacks(0, 1)
                if has(r):
                    sp.wait_ge(lin_sb, 2 * (r + 1))
                    if r >= 1:
                        sp.wait_ge(inv_s, r)
                    den_rows(lin, 1, den_lin_in)
                    load_max(r)
                if has(r) and has(r + 1):
                    load_stacks(r + 1, 0)
                    load_stacks(r + 1, 1)
                if has(r):
                    sp.wait_ge(att_sb, 2 * (r + 1))
                    den_rows(att, 0, den_in)
                    sp.wait_ge(ginv_s, 2 * (r + 1))
                    if r == 0:
                        sp.wait_ge(w13_lo_s, 1)
                    else:
                        sp.wait_ge(rden_in, 32 * r)
                    for k in range(2):
                        sp.dma_start(ginv_rows[:, k, :], ginv[:, k, :]).then_inc(ginv_row, 16)
                    sp.wait_ge(ginv_row, 32 * (r + 1))
                    if r == 0:
                        sp.wait_ge(had_ps, 4)
                    else:
                        sp.wait_ge(norm_lin, r)
                        sp.wait_ge(norm_att, r)
                    for k in range(2):
                        sp.dma_start(rden[:, k, :],
                                     ginv_rows[:, k, :].unsqueeze(1).broadcast_to([4, STRIP, NG * S])).then_inc(rden_in, 16)
                if has(r - 1):
                    sp.wait_ge(y_s, r)
                    sp.dma_start(xv(out, r - 1), xs[:, r - 1]).then_inc(y_out, 16)
            sp.wait_ge(y_out, 16 * NB)
            sp.wait_ge(parts_out, 32 * NB)

        @block.scalar
        def _(act):
            act.dma_start(wqkv_raw[:, 2], wvT.rearrange("(c p) n -> p c n", p=P)).then_inc(wqkv_in, 16)
            act.dma_start(cst[:], const).then_inc(const_in, 16)
            act.dma_start(gcol[:], gate).then_inc(gate_in, 16)
            act.wait_ge(wo_zero, 1)
            for j in range(4):
                act.dma_start(wo[STRIP * j:STRIP * j + HD, :, :],
                              woT.rearrange("(g j e) n -> j e g n", j=4, e=HD)[j]).then_inc(wo_in, 16)
            act.wait_ge(wqkv_in, 48)
            act.activation(wqkv_hi[:], wqkv_raw, ACT.Copy).then_inc(wqkv_hi_s, 1)

            def evac_hT(b):
                act.wait_ge(hT_ps, b + 1)
                if b >= 1:
                    act.wait_ge(v_ps, b)
                act.activation(hT_hi[:], misc_bank[0][:], ACT.Copy).then_inc(hT_hi_s, 1)

            def split_parts(b):
                act.wait_ge(rope_sum, 2 * (b + 1))
                if b >= 1:
                    act.wait_ge(parts_out, 32 * b)
                act.activation(part_hi[:], roped[:], ACT.Copy).then_inc(part_hi_s, 1)

            def evac_v(b):
                act.wait_ge(v_ps, b + 1)
                if b < 2:
                    act.wait_ge(v_const, 4)
                else:
                    act.wait_ge(pv_group, NG * (b - 1))
                act.activation(v_strips[b % 2][:, :, :, 0:HD],
                               misc_bank[0][:].rearrange("p t (h e) -> p t h e", e=HD), ACT.Copy).then_inc(v_sb, 1)

            def exp_elu(b):
                act.wait_ge(neg_s, b + 1)
                act.activation(elu, elu, ACT.Exp).then_inc(elu_s, 1)

            def evac_kfT(b):
                act.wait_ge(kfT_ps, b + 1)
                if b >= 1:
                    act.wait_ge(mem_ps, b)
                act.activation(kfT[:], misc_bank[0][:], ACT.Copy).then_inc(kfT_sb, 1)

            def evac_lin(b):
                for u in range(2):
                    act.wait_ge(lin_ps, 2 * b + u + 1)
                    if b == 0:
                        act.wait_ge(w13_lo_s, 1)
                    else:
                        act.wait_ge(comb_s, b)
                    act.activation(lin[:, 2 * u:2 * u + 2, :], misc_bank[u][:], ACT.Copy).then_inc(lin_sb, 1)

            def split_max(b):
                act.wait_ge(maxT_ps, b + 1)
                if b >= 1:
                    act.wait_ge(maxrow_in, 64 * b)
                act.activation(nmT_hi[:], misc_bank[1][0:TT * NH, 0, 0:P], ACT.Copy, scale=-1.0).then_inc(nm_hi_s, 1)

            def exp_head(b, h):
                act.wait_ge(exp_ps, NH * b + h + 1)
                if b == 0 and h == 0:
                    act.wait_ge(w2_lo_s, 1)
                if NH * b + h >= 8:
                    act.wait_ge(pv_group, (NH * b + h - 8) // 4 + 1)
                act.activation(prob[:, h % 8], exp_bank[h % 2][:], ACT.Exp, scale=SCALE).then_inc(prob_s, 1)

            def evac_att(b, u):
                act.wait_ge(pv_group, NG * b + 2 * u + 2)
                if b >= 1:
                    act.wait_ge(wo_ps, b)
                act.activation(att[:, 2 * u:2 * u + 2, :], pv_bank[:], ACT.Copy).then_inc(att_sb, 1)

            def evac_h2T(b):
                act.wait_ge(h2T_ps, b + 1)
                if b >= 1:
                    act.wait_ge(up_ps, FC * b)
                act.activation(h2T_hi[:], misc_bank[0][:], ACT.Copy).then_inc(h2T_hi_s, 1)

            def ffn_tanh(b, c):
                n = FC * b + c
                act.wait_ge(up_ps, n + 1)
                if n == 0:
                    act.wait_ge(w13_lo_s, 1)
                if n >= 3:
                    act.wait_ge(hid_hi_s, n - 2)
                    act.wait_ge(hid_lo_s, n - 2)
                act.activation(ffn_work[n % 3], score_bank[c % 2][:, 0, :], ACT.Tanh, scale=0.5).then_inc(tanh_s, 1)

            def split_hid(b, c):
                n = FC * b + c
                act.wait_ge(hid_s, n + 1)
                if n >= 3:
                    act.wait_ge(down_ps, n - 2)
                act.activation(hid_hi[:, n % 3, :], ffn_work[n % 3], ACT.Copy).then_inc(hid_hi_s, 1)

            def split_wide():
                act.wait_ge(w13_in, 32)
                act.activation(w13_hi[:], wide_raw[:], ACT.Copy).then_inc(w13_hi_s, 1)

            def prepare_w2():
                act.wait_ge(gate_in, 16)
                act.activation(gexp[:], gcol[:], ACT.Exp, scale=-1.0).then_inc(gate_exp, 1)
                for u, src in enumerate((score_bank[0], score_bank[1], exp_bank[0], exp_bank[1])):
                    act.wait_ge(had_ps, u + 1)
                    act.activation(w2_a[:, 2 * u:2 * u + 2, :], src[:], ACT.Copy, scale=1.0 / 64).then_inc(had_sb, 1)
                act.wait_ge(fly, 6)
                act.activation(w2_hi[:], w2_b, ACT.Copy).then_inc(w2_hi_s, 1)

            evac_hT(0)
            for r in ROUNDS:
                if has(r + 1):
                    split_parts(r + 1)
                    evac_v(r + 1)
                if r < 0:
                    split_wide()
                if has(r):
                    evac_lin(r)
                    split_max(r)
                if has(r - 1):
                    evac_h2T(r - 1)
                    for c in range(4):
                        ffn_tanh(r - 1, c)
                        split_hid(r - 1, c)
                for g in range(NG):
                    if has(r):
                        for h in range(4 * g, 4 * g + 4):
                            exp_head(r, h)
                        if g == 2:
                            evac_att(r, 0)
                    if has(r - 1):
                        ffn_tanh(r - 1, 4 + g)
                        split_hid(r - 1, 4 + g)
                    if g == 1 and has(r + 1):
                        exp_elu(r + 1)
                if has(r):
                    evac_att(r, 1)
                if has(r + 1):
                    evac_kfT(r + 1)
                if has(r + 2):
                    evac_hT(r + 2)
                if r < 0:
                    prepare_w2()

        @block.gpsimd
        def _(pool):
            pool.memset(mhalf[:], -0.5).then_inc(mhalf_set, 1)
            pool.memset(wo[:], 0.0).then_inc(wo_zero, 1)
            pool.memset(q_stack[:].bitcast(F32), 0.0).then_inc(stack_zero, 1)

            def ln_power(n):
                if n == 0:
                    pool.wait_ge(mhalf_set, 1)
                pool.wait_ge(ln_ve, n + 1)
                if n >= 1:
                    pool.wait_ge(ln_xn, TT * n)
                pool.tensor_tensor(rstd[:], var_eps[:], mhalf[:], ALU.pow).then_inc(ln_rstd, 1)

            def rope_sums(b):
                if b >= 1:
                    pool.wait_ge(feat_s, b)
                    pool.wait_ge(part_hi_s, b)
                    pool.wait_ge(part_lo_s, b)
                pool.wait_ge(rope_prod, 4 * b + 2)
                pool.tensor_tensor(roped[:, 0], prod[:, 0], prod[:, 1], ALU.subtract).then_inc(rope_sum, 1)
                pool.wait_ge(rope_prod, 4 * b + 4)
                pool.tensor_tensor(roped[:, 1], prod[:, 2], prod[:, 3], ALU.add).then_inc(rope_sum, 1)

            def hid_low(b, c):
                n = FC * b + c
                pool.wait_ge(hid_hi_s, n + 1)
                if n >= 3:
                    pool.wait_ge(down_ps, n - 2)
                pool.tensor_tensor(hid_lo[:, n % 3, :], ffn_work[n % 3], hid_hi[:, n % 3, :].bitcast(F32),
                                   ALU.subtract).then_inc(hid_lo_s, 1)

            def norm_linear(b):
                pool.wait_ge(rden_in, 32 * (b + 1))
                pool.wait_ge(den_lin_in, 16 * (b + 1))
                v = lin.rearrange("p g n -> p (g n)")
                pool.tensor_tensor(v, v, rden[:, 1, :], ALU.mult).then_inc(norm_lin, 1)

            ln_power(0)
            ln_power(1)
            pool.memset(k_stack[:].bitcast(F32), 0.0).then_inc(k_zero, 1)
            pool.wait_ge(k_zero, 1)
            pool.memset(k_stack[MAXROW:MAXROW + 2].bitcast(F32), 1.0).then_inc(stack_zero, 1)
            pool.wait_ge(stack_zero, 2)
            rope_sums(0)
            for r in ROUNDS:
                if has(r + 1) and r >= 0:
                    rope_sums(r + 1)
                if r < 0:
                    pool.wait_ge(w13_hi_s, 1)
                    pool.tensor_tensor(w13_lo[:], wide_raw[:], w13_hi[:].bitcast(F32), ALU.subtract).then_inc(w13_lo_s, 1)
                if has(r - 1):
                    norm_linear(r - 1)
                    ln_power(LN[(2, r - 1)])
                    for c in range(FC):
                        hid_low(r - 1, c)
                if has(r + 2) and r >= 0:
                    ln_power(LN[(1, r + 2)])

        @block.vector
        def _(dve):
            for k in range(2):
                dve.memset(v_strips[k][:], 0.0).then_inc(v_const, 1)
            dve.memset(mem[:], 0.0).then_inc(mem_zero, 1)
            dve.wait_ge(v_const, 2)
            for k in range(2):
                dve.memset(v_strips[k][:, :, :, HD:VW], 1.0).then_inc(v_const, 1)

            def ln_statistics(n):
                which, b = LN_ORDER[n]
                if which == 1:
                    dve.wait_ge(x_in[b], 16)
                else:
                    dve.wait_ge(x2_s, b + 1)
                if n >= 1:
                    dve.wait_ge(ln_mv, TT * n)
                for tt in range(TT):
                    dve.bn_stats(stats[:, tt, :], xs[:, b, tt, :]).then_inc(ln_stats, 1)
                if n >= 1:
                    dve.wait_ge(ln_xn, TT * n)
                for tt in range(TT):
                    dve.wait_ge(ln_stats, TT * n + tt + 1)
                    dve.bn_aggr(mv[:, tt, :], stats[:, tt, :]).then_inc(ln_mv, 1)
                dve.wait_ge(ln_mv, TT * (n + 1))
                if n >= 1:
                    dve.wait_ge(ln_rstd, n)
                dve.tensor_scalar(var_eps[:], mv[:, :, 1], EPS, None, ALU.add).then_inc(ln_ve, 1)

            def ln_normalise(n):
                which, b = LN_ORDER[n]
                dve.wait_ge(ln_rstd, n + 1)
                if n >= 1:
                    dve.wait_ge(*xn_read(n - 1))
                for tt in range(TT):
                    dve.tensor_scalar(xn[:, tt, :], xs[:, b, tt, :], mv[:, tt, 0:1], rstd[:, tt:tt + 1],
                                      ALU.subtract, ALU.mult).then_inc(ln_xn, 1)

            def low_hT(b):
                dve.wait_ge(hT_hi_s, b + 1)
                dve.tensor_tensor(hT_lo[:], misc_bank[0][:], hT_hi[:].bitcast(F32), ALU.subtract).then_inc(hT_lo_s, 1)

            def low_h2T(b):
                dve.wait_ge(h2T_hi_s, b + 1)
                dve.tensor_tensor(h2T_lo[:], misc_bank[0][:], h2T_hi[:].bitcast(F32), ALU.subtract).then_inc(h2T_lo_s, 1)

            def row_maxima(b, heads):
                for h in heads:
                    n = NH * b + h
                    dve.wait_ge(score_ps, n + 1)
                    if h == 0 and b >= 1:
                        dve.wait_ge(maxT_ps, b)
                    dve.tensor_reduce(rowmax[:, :, h], score_bank[h % 2][:], AX.X, ALU.max).then_inc(rowmax_s, 1)

            def rope_products(b):
                if b == 0:
                    dve.wait_ge(const_in, 16)
                else:
                    dve.wait_ge(rope_sum, 2 * b)
                    dve.wait_ge(feat_s, b)
                dve.wait_ge(qk_ps, 2 * (b + 1))
                for k, (c, table) in enumerate(((0, cos2), (1, sin2), (1, cos2), (0, sin2))):
                    dve.tensor_tensor(prod[:, k], misc_bank[c][:], table, ALU.mult).then_inc(rope_prod, 1)

            def low_parts(b):
                dve.wait_ge(part_hi_s, b + 1)
                if b >= 1:
                    dve.wait_ge(parts_out, 32 * b)
                dve.tensor_tensor(part_lo[:], roped[:], part_hi[:].bitcast(F32), ALU.subtract).then_inc(part_lo_s, 1)

            def negative_part(b):
                dve.wait_ge(rope_sum, 2 * (b + 1))
                dve.tensor_scalar(elu, roped[:], 0.0, None, ALU.min).then_inc(neg_s, 1)

            def features(b):
                dve.wait_ge(elu_s, b + 1)
                if b >= 1:
                    dve.wait_ge(lin_ps, 2 * b)
                dve.scalar_tensor_tensor(out=feat[:].rearrange("p c m n -> p (c m n)"),
                                         in0=roped[:].rearrange("p c m n -> p (c m n)"), scalar=1.0,
                                         in1=elu.rearrange("p c m n -> p (c m n)"),
                                         op0=ALU.add, op1=ALU.max).then_inc(feat_s, 1)

            def memory_strips(b):
                dve.wait_ge(mem_ps, b + 1)
                if b == 0:
                    dve.wait_ge(mem_zero, 1)
                else:
                    dve.wait_ge(lin_ps, 2 * b)
                for c in range(DC):
                    dve.tensor_tensor(mem[:, c, :, 0:VW],
                                      misc_bank[1][:, c, 0:HH * VW].rearrange("p (h e) -> p h e", e=VW),
                                      mask, ALU.mult).then_inc(mem_sb, 1)

            def normalise(b):
                dve.wait_ge(rden_in, 32 * (b + 1))
                dve.wait_ge(den_in, 16 * (b + 1))
                v = att[:].rearrange("p g n -> p (g n)")
                dve.tensor_tensor(v, v, rden[:, 0, :], ALU.mult).then_inc(norm_att, 1)
                dve.wait_ge(norm_att, b + 1)
                dve.wait_ge(norm_lin, b + 1)
                dve.tensor_tensor(att[:], att[:], lin, ALU.add).then_inc(comb_s, 1)

            def first_residual(b):
                dve.wait_ge(wo_ps, b + 1)
                dve.tensor_tensor(xs[:, b], xs[:, b], misc_bank[1][:], ALU.add).then_inc(x2_s, 1)

            def low_max(b):
                dve.wait_ge(nm_hi_s, b + 1)
                if b >= 1:
                    dve.wait_ge(maxrow_in, 64 * b)
                dve.scalar_tensor_tensor(out=nmT_lo[:], in0=misc_bank[1][0:TT * NH, 0, 0:P], scalar=-1.0,
                                         in1=nmT_hi[:].bitcast(F32), op0=ALU.mult, op1=ALU.subtract).then_inc(nm_lo_s, 1)

            def ffn_gate(b, c):
                n = FC * b + c
                work = ffn_work[n % 3]
                dve.wait_ge(tanh_s, n + 1)
                dve.scalar_tensor_tensor(out=work, in0=work, scalar=1.0, in1=score_bank[c % 2][:, 0, :],
                                         op0=ALU.add, op1=ALU.mult).then_inc(gated_s, 1)
                dve.wait_ge(gated_s, n + 1)
                dve.tensor_tensor(work, work, score_bank[c % 2][:, 1, :], ALU.mult).then_inc(hid_s, 1)

            def reciprocals(b):
                dve.wait_ge(den_in, 16 * (b + 1))
                dve.wait_ge(den_lin_in, 16 * (b + 1))
                if b == 0:
                    dve.wait_ge(gate_s, 3)
                else:
                    dve.wait_ge(ginv_s, 2 * b)
                dve.reciprocal(inv[:], den[:]).then_inc(inv_s, 1)
                dve.wait_ge(inv_s, b + 1)
                if b >= 1:
                    dve.wait_ge(ginv_row, 32 * b)
                for k in range(2):
                    dve.tensor_scalar(ginv[:, k, :], inv[:, k, :], gate2[:, k:k + 1], None, ALU.mult).then_inc(ginv_s, 1)

            def second_residual(b):
                dve.wait_ge(down_ps, FC * (b + 1))
                dve.wait_ge(ln_xn, TT * (LN[(2, b)] + 1))
                dve.tensor_tensor(xs[:, b], xs[:, b], down_bank[:], ALU.add).then_inc(y_s, 1)

            def prepare_weights():
                dve.wait_ge(gate_exp, 1)
                dve.tensor_scalar(gsum[:], gexp[:], 1.0, None, ALU.add).then_inc(gate_s, 1)
                dve.wait_ge(gate_s, 1)
                dve.reciprocal(gate2[:, 1:2], gsum[:]).then_inc(gate_s, 1)
                dve.wait_ge(gate_s, 2)
                dve.tensor_scalar(gate2[:, 0:1], gate2[:, 1:2], -1.0, 1.0, ALU.mult, ALU.add).then_inc(gate_s, 1)
                dve.wait_ge(had_sb, 4)
                for s, (src, dst) in enumerate(((w2_a, w2_b), (w2_b, w2_a), (w2_a, w2_b))):
                    if s >= 1:
                        dve.wait_ge(fly, 2 * s)
                    i, o = (v.rearrange("p (o k i) n -> p o k (i n)", k=2, i=4 >> s) for v in (src, dst))
                    for k, op in enumerate((ALU.add, ALU.subtract)):
                        dve.tensor_tensor(o[:, :, k], i[:, :, 0], i[:, :, 1], op).then_inc(fly, 1)
                dve.wait_ge(w2_hi_s, 1)
                dve.tensor_tensor(w2_lo[:], w2_b, w2_hi[:].bitcast(F32), ALU.subtract).then_inc(w2_lo_s, 1)

            ln_statistics(0)
            dve.wait_ge(wqkv_hi_s, 1)
            ln_normalise(0)
            dve.tensor_tensor(wqkv_lo[:], wqkv_raw, wqkv_hi[:].bitcast(F32), ALU.subtract).then_inc(wqkv_lo_s, 1)
            low_hT(0)
            ln_statistics(1)
            for r in ROUNDS:
                if has(r):
                    row_maxima(r, range(0, 4))
                if has(r + 1):
                    rope_products(r + 1)
                if has(r):
                    row_maxima(r, range(4, 8))
                if has(r + 1):
                    low_parts(r + 1)
                if has(r - 1):
                    normalise(r - 1)
                if has(r):
                    row_maxima(r, range(8, 12))
                if has(r - 1):
                    first_residual(r - 1)
                    ln_statistics(LN[(2, r - 1)])
                if has(r):
                    row_maxima(r, range(12, 16))
                if has(r - 1):
                    ln_normalise(LN[(2, r - 1)])
                    low_h2T(r - 1)
                if has(r):
                    low_max(r)
                if has(r - 1):
                    for c in range(4):
                        ffn_gate(r - 1, c)
                for g in range(NG):
                    if g == 0 and has(r + 1):
                        negative_part(r + 1)
                    if has(r - 1):
                        ffn_gate(r - 1, 4 + g)
                    if g == 2 and has(r + 1):
                        features(r + 1)
                if has(r + 2) and r >= 0:
                    ln_statistics(LN[(1, r + 2)])
                if has(r - 1):
                    second_residual(r - 1)
                if has(r + 1):
                    memory_strips(r + 1)
                if has(r + 2):
                    ln_normalise(LN[(1, r + 2)])
                    low_hT(r + 2)
                if r < 0:
                    prepare_weights()
                if has(r):
                    reciprocals(r)

        @block.tensor
        def _(pe):
            free = {}

            def claim(bank):
                if bank.name in free:
                    pe.wait_ge(*free[bank.name])
                return bank

            def three(out_ap, lhs, rhs, start, stop, **kw):
                pe.matmul(out_ap, lhs[0], rhs[0], start=start, stop=False, **kw)
                pe.matmul(out_ap, lhs[0], rhs[1], start=False, stop=False, **kw)
                return pe.matmul(out_ap, lhs[1], rhs[0], start=False, stop=stop, **kw)

            def transpose_rows(n):
                which, b = LN_ORDER[n]
                done, reader = ((hT_ps, hT_lo_s), (h2T_ps, h2T_lo_s))[which - 1]
                if n == 0:
                    pe.wait_ge(const_in, 16)
                pe.wait_ge(ln_xn, TT * (n + 1))
                bank = claim(misc_bank[0])
                for c in range(DC):
                    for tt in range(TT):
                        mm = pe.transpose(bank[:, c, tt * P:tt * P + P], xn[:, tt, c * P:c * P + P], ident)
                mm.then_inc(done, 1)
                free[bank.name] = (reader, b + 1)

            def project_qk(b):
                if b == 0:
                    pe.wait_ge(wqkv_hi_s, 1)
                    pe.wait_ge(wqkv_lo_s, 1)
                pe.wait_ge(hT_hi_s, b + 1)
                pe.wait_ge(hT_lo_s, b + 1)
                for c in range(DC):
                    bank = claim(misc_bank[c])
                    for m in range(2):
                        for k in range(DC):
                            cols = slice(c * P, c * P + P)
                            mm = three(bank[:, m, :], (wqkv_hi[:, m, k, cols], wqkv_lo[:, m, k, cols]),
                                       (hT_hi[:, k, :], hT_lo[:, k, :]), k == 0, k == DC - 1)
                    mm.then_inc(qk_ps, 1)
                    free[bank.name] = (rope_prod, 4 * (b + 1))

            def project_v(b):
                bank = claim(misc_bank[0])
                for tt in range(TT):
                    rows = slice(tt * P, tt * P + P)
                    for k in range(DC):
                        mm = three(bank[:, tt, :], (hT_hi[:, k, rows], hT_lo[:, k, rows]),
                                   (wqkv_hi[:, 2, k, :], wqkv_lo[:, 2, k, :]), k == 0, k == DC - 1)
                mm.then_inc(v_ps, 1)
                free[bank.name] = (v_sb, b + 1)

            def scores(b, heads):
                for h in heads:
                    if h % HH == 0:
                        pe.wait_ge(stack_in[h // HH], 96 * (b + 1))
                    bank = claim(score_bank[h % 2])
                    for tt in range(TT):
                        mm = pe.matmul(bank[:, tt, :], q_stack[0:MAXROW, h, tt * P:tt * P + P], k_stack[0:MAXROW, h, :],
                                       start=True, stop=True)
                    mm.then_inc(score_ps, 1)
                    free[bank.name] = (rowmax_s, NH * b + h + 1)

            def transpose_max(b):
                pe.wait_ge(rowmax_s, NH * (b + 1))
                bank = claim(misc_bank[1])
                pe.transpose(bank[0:TT * NH, 0, 0:P], rowmax[:].rearrange("p t h -> p (t h)"), ident).then_inc(maxT_ps, 1)
                free[bank.name] = (nm_lo_s, b + 1)

            def shifted_scores(b, h):
                if h == 0:
                    pe.wait_ge(maxrow_in, 64 * (b + 1))
                bank = claim(exp_bank[h % 2])
                for tt in range(TT):
                    mm = pe.matmul(bank[:, tt, :], k_stack[:, h, tt * P:tt * P + P], q_stack[:, h, :],
                                   start=True, stop=True)
                mm.then_inc(exp_ps, 1)
                free[bank.name] = (prob_s, NH * b + h + 1)

            def product_v(b, g):
                if g == 0:
                    pe.wait_ge(v_sb, b + 1)
                pe.wait_ge(prob_s, NH * b + 4 * g + 4)
                bank = claim(pv_bank) if g % 2 == 0 else pv_bank
                for tt in range(TT):
                    for j in range(4):
                        h = 4 * g + j
                        mm = pe.matmul(bank[STRIP * j:STRIP * j + STRIP, g % 2, :], v_strips[b % 2][:, tt, h, :],
                                       prob[:, h % 8, tt, :], start=(tt == 0), stop=(tt == TT - 1))
                mm.then_inc(pv_group, 1)
                free[bank.name] = (att_sb, 2 * b + g // 2 + 1)

            def memory(b):
                pe.wait_ge(feat_s, b + 1)
                bank = claim(misc_bank[0])
                for tt in range(TT):
                    for c in range(DC):
                        mm = pe.transpose(bank[:, tt, c * P:c * P + P], feat[:, c, 1, tt * P:tt * P + P], ident)
                mm.then_inc(kfT_ps, 1)
                free[bank.name] = (kfT_sb, b + 1)
                pe.wait_ge(kfT_sb, b + 1)
                pe.wait_ge(v_sb, b + 1)
                bank = claim(misc_bank[1])
                for c in range(DC):
                    for tt in range(TT):
                        mm = pe.matmul(bank[:, c, 0:HH * VW], kfT[:, tt, c * P:c * P + P],
                                       v_strips[b % 2][:, tt, HH * c:HH * c + HH, 0:VW],
                                       start=(tt == 0), stop=(tt == TT - 1))
                mm.then_inc(mem_ps, 1)
                free[bank.name] = (mem_sb, 2 * (b + 1))

            def read_memory(b):
                pe.wait_ge(mem_sb, 2 * (b + 1))
                for c in range(DC):
                    bank = claim(misc_bank[c])
                    for u in range(2):
                        mm = pe.matmul(bank[:, u, :], mem[:, c, 4 * u:4 * u + 4, :].rearrange("p h e -> p (h e)"),
                                       feat[:, c, 0, :], start=True, stop=True)
                    mm.then_inc(lin_ps, 1)
                    free[bank.name] = (lin_sb, 2 * b + c + 1)

            def project_out(b):
                if b == 0:
                    pe.wait_ge(wo_in, 64)
                pe.wait_ge(comb_s, b + 1)
                bank = claim(misc_bank[1])
                for tt in range(TT):
                    for g in range(NG):
                        mm = pe.matmul(bank[:, tt, :], att[:, g, tt * P:tt * P + P], wo[:, g, :],
                                       start=(g == 0), stop=(g == NG - 1))
                mm.then_inc(wo_ps, 1)
                free[bank.name] = (x2_s, b + 1)

            def ffn_up(b, c):
                if c == 0:
                    if b == 0:
                        pe.wait_ge(w13_hi_s, 1)
                        pe.wait_ge(w13_lo_s, 1)
                    pe.wait_ge(h2T_hi_s, b + 1)
                    pe.wait_ge(h2T_lo_s, b + 1)
                bank = claim(score_bank[c % 2])
                cols = slice(c * P, c * P + P)
                for m in range(2):
                    for k in range(DC):
                        mm = three(bank[:, m, :], (w13_hi[:, m, k, cols], w13_lo[:, m, k, cols]),
                                   (h2T_hi[:, k, :], h2T_lo[:, k, :]), k == 0, k == DC - 1)
                mm.then_inc(up_ps, 1)
                free[bank.name] = (hid_s, FC * b + c + 1)

            def ffn_down(b, c):
                n = FC * b + c
                if n == 0:
                    pe.wait_ge(w2_hi_s, 1)
                    pe.wait_ge(w2_lo_s, 1)
                pe.wait_ge(hid_hi_s, n + 1)
                pe.wait_ge(hid_lo_s, n + 1)
                bank = claim(down_bank) if c == 0 else down_bank
                for tt in range(TT):
                    rows = slice(tt * P, tt * P + P)
                    mm = three(bank[:, tt, :], (hid_hi[:, n % 3, rows], hid_lo[:, n % 3, rows]),
                               (w2_hi[:, c, :], w2_lo[:, c, :]), c == 0 and tt == 0, c == FC - 1,
                               skip_group_check=True)
                mm.then_inc(down_ps, 1)
                free[bank.name] = (y_s, b + 1)

            def ffn(b, c):
                if c < FC:
                    ffn_up(b, c)
                if c >= 2:
                    ffn_down(b, c - 2)

            def hadamard():
                pe.wait_ge(w2_in, 16)
                for u, bank in enumerate((score_bank[0], score_bank[1], exp_bank[0], exp_bank[1])):
                    for k in range(2):
                        mm = pe.matmul(bank[:, k, :], had, w2_raw[:, 2 * u + k, :], start=True, stop=True)
                    mm.then_inc(had_ps, 1)
                    free[bank.name] = (had_sb, u + 1)

            transpose_rows(0)
            for r in ROUNDS:
                if has(r):
                    scores(r, range(0, 4))
                if has(r + 1):
                    project_qk(r + 1)
                if has(r):
                    scores(r, range(4, 8))
                if has(r + 1):
                    project_v(r + 1)
                if has(r):
                    scores(r, range(8, 12))
                if has(r - 1):
                    project_out(r - 1)
                if has(r):
                    read_memory(r)
                    scores(r, range(12, 16))
                if has(r - 1):
                    transpose_rows(LN[(2, r - 1)])
                if has(r):
                    transpose_max(r)
                if has(r - 1):
                    for c in range(4):
                        ffn(r - 1, c)
                for g in range(NG):
                    if has(r):
                        for h in range(4 * g, 4 * g + 4):
                            shifted_scores(r, h)
                        if g >= 1:
                            product_v(r, g - 1)
                    if has(r - 1):
                        ffn(r - 1, 4 + g)
                if has(r):
                    product_v(r, NG - 1)
                if has(r - 1):
                    ffn(r - 1, FC)
                    ffn(r - 1, FC + 1)
                if has(r + 1):
                    memory(r + 1)
                if has(r + 2):
                    transpose_rows(LN[(1, r + 2)])
                if r < 0:
                    hadamard()


def kernel(L0_attn_hidden_states, L0_attn_Wq, L0_attn_Wk, L0_attn_Wv, L0_attn_Wo, L0_attn_gate,
           L0_ffn_W1, L0_ffn_W2, L0_ffn_W3):
    import concourse.bacc as bacc
    from concourse.bass_utils import run_bass_kernel_spmd

    def turned(w):
        return np.ascontiguousarray(np.asarray(w).T)

    gates = np.ascontiguousarray(np.repeat(np.asarray(L0_attn_gate).reshape(NG, 4).T.reshape(NH, 1), P // NH, axis=0))
    arrays = {
        "x": np.ascontiguousarray(L0_attn_hidden_states),
        "wqT": turned(L0_attn_Wq), "wkT": turned(L0_attn_Wk), "wvT": turned(L0_attn_Wv), "woT": turned(L0_attn_Wo),
        "gate": gates,
        "w1T": turned(L0_ffn_W1), "w3T": turned(L0_ffn_W3), "w2T": turned(L0_ffn_W2),
        "const": shape_constants(),
    }
    nc = bacc.Bacc("TRN2", target_bir_lowering=False, num_devices=1)
    aps = [nc.dram_tensor(f"in_{n}", a.shape, F32, kind="ExternalInput").ap() for n, a in arrays.items()]
    out = nc.dram_tensor("out_y", (NB, S, D), F32, kind="ExternalOutput").ap()
    build(nc, *aps, out)
    r = run_bass_kernel_spmd(nc, [{f"in_{n}": a for n, a in arrays.items()}], core_ids=[0])
    return r.results[0]["out_y"]
```

```python
from contextlib import ExitStack

import numpy as np

import concourse.bass as bass
from concourse import mybir

F32 = mybir.dt.float32
F32R = mybir.dt.float32r
ALU = mybir.AluOpType
ACT = mybir.ActivationFunctionType
AX = mybir.AxisListType

P = 128
NB, S, D = 4, 256, 256
NH, HD = 16, 16
FF = 1024
TT = S // P
DC = D // P
FC = FF // P
NG = NH // 4
HH = NH // DC
STRIP = 32
VW = HD + 1
MAXROW = 64
EPS = 1e-5
SCALE = HD ** -0.5
C_ID, C_HAD, C_COS, C_SIN, C_MASK = 0, P, 2 * P, 2 * P + S, 2 * P + 2 * S
NCONST = C_MASK + HH


def shape_constants():
    i = np.arange(P)
    bits = i[:, None] & i[None, :]
    parity = np.zeros_like(bits)
    for s in range(7):
        parity ^= (bits >> s) & 1
    inv_freq = (1.0 / np.float32(10000.0) ** (np.arange(0, D, 2, dtype=np.float32) / np.float32(D))).astype(np.float32)
    angle = inv_freq[:, None] * np.arange(S, dtype=np.float32)[None, :]
    c = np.zeros((P, NCONST), np.float32)
    c[:, C_ID:C_ID + P] = np.eye(P)
    c[:, C_HAD:C_HAD + P] = 1 - 2 * parity
    c[:, C_COS:C_COS + S] = np.cos(angle)
    c[:, C_SIN:C_SIN + S] = np.sin(angle)
    c[:, C_MASK:C_MASK + HH] = (i[:, None] // HD == np.arange(HH)[None, :])
    return c


def build(nc, x, wqT, wkT, wvT, woT, gate, w1T, w3T, w2T, const, out):
    with ExitStack() as ctx:
        def sb(name, shape, dt=F32):
            return ctx.enter_context(nc.sbuf_tensor(name, shape, dt))

        def sem(name):
            return ctx.enter_context(nc.semaphore(name))

        def bank(name):
            return ctx.enter_context(nc.psum_tensor(name, [P, 2, 256], F32))

        score_bank = [bank("score_bank0"), bank("score_bank1")]
        exp_bank = [bank("exp_bank0"), bank("exp_bank1")]
        pv_bank = bank("pv_bank")
        misc_bank = [bank("misc_bank0"), bank("misc_bank1")]
        down_bank = bank("down_bank")

        xs = sb("xs", [P, NB, TT, D])
        cst = sb("cst", [P, NCONST])
        ident = cst[:, C_ID:C_ID + P]
        had = cst[:, C_HAD:C_HAD + P]
        cos2 = cst[:, C_COS:C_COS + S].unsqueeze(1).broadcast_to([P, 2, S])
        sin2 = cst[:, C_SIN:C_SIN + S].unsqueeze(1).broadcast_to([P, 2, S])
        mask = cst[:, C_MASK:C_MASK + HH].unsqueeze(2).broadcast_to([P, HH, VW])
        wide_raw = sb("wide_raw", [P, 2, DC, FF])
        narrow_raw = sb("narrow_raw", [P, 2048])
        wqkv_raw = narrow_raw[:, 0:3 * DC * D].rearrange("p (m c n) -> p m c n", m=3, c=DC)
        w2_raw = narrow_raw[:, :].rearrange("p (c n) -> p c n", c=FC)
        w2_b = wide_raw[:, 1, :, :].rearrange("p c (k n) -> p (c k) n", n=D)
        den_cols = narrow_raw[:, 0:NG * S]
        rden = narrow_raw[:, NG * S:]
        ffn_work = [wide_raw[:, 0, 0, 256 * k:256 * k + 256] for k in range(3)]
        wqkv_hi = sb("wqkv_hi", [P, 3, DC, D], F32R)
        wqkv_lo = sb("wqkv_lo", [P, 3, DC, D], F32R)
        w13_hi = sb("w13_hi", [P, 2, DC, FF], F32R)
        w13_lo = sb("w13_lo", [P, 2, DC, FF], F32R)
        w2_hi = sb("w2_hi", [P, FC, D], F32R)
        w2_lo = sb("w2_lo", [P, FC, D], F32R)
        wo = sb("wo", [P, NG, D])
        stats = sb("stats", [P, TT, 6])
        mv = sb("mv", [P, TT, 2])
        var_eps = sb("var_eps", [P, TT])
        rstd = sb("rstd", [P, TT])
        mhalf = sb("mhalf", [P, TT])
        xn = sb("xn", [P, TT, D])
        hT_hi = sb("hT_hi", [P, DC, S], F32R)
        hT_lo = sb("hT_lo", [P, DC, S], F32R)
        h2T_hi = sb("h2T_hi", [P, DC, S], F32R)
        h2T_lo = sb("h2T_lo", [P, DC, S], F32R)
        prod = sb("prod", [P, 4, 2, S])
        elu = prod[:, 0:2, :, :]
        roped = sb("roped", [P, DC, 2, S])
        part_hi = sb("part_hi", [P, DC, 2, S], F32R)
        part_lo = sb("part_lo", [P, DC, 2, S], F32R)
        feat = sb("feat", [P, DC, 2, S])
        q_stack = sb("q_stack", [P, NH, S], F32R)
        k_stack = sb("k_stack", [P, NH, S], F32R)
        v_strips = [sb("v_strips0", [P, TT, NH, STRIP]), sb("v_strips1", [P, TT, NH, STRIP])]
        kfT = sb("kfT", [P, TT, D])
        mem = sb("mem", [P, DC, HH, STRIP])
        rowmax = sb("rowmax", [P, NH, TT])
        nmT_hi = sb("nmT_hi", [TT * NH, P], F32R)
        nmT_lo = sb("nmT_lo", [TT * NH, P], F32R)
        prob = sb("prob", [P, 8, TT, S])
        att = sb("att", [P, NG, S])
        lin = wide_raw[:, 0, 1, :].rearrange("p (g n) -> p g n", g=NG)
        inv = sb("inv", [P, NG, S // STRIP])
        ginv = sb("ginv", [P, NG, S // STRIP])
        gcol = sb("gcol", [P, NG])
        gexp = sb("gexp", [P, NG])
        gsum = sb("gsum", [P, NG])
        gate2 = sb("gate2", [P, 2, NG])
        hid_hi = sb("hid_hi", [P, 3, S], F32R)
        hid_lo = sb("hid_lo", [P, 3, S], F32R)
        parts = nc.dram_tensor("parts", [NB, 2, DC, 2, P, S], F32, kind="Internal").ap()

        x_in = [sem(f"x_in{b}") for b in range(NB)]
        wqkv_in = [sem(f"w{m}_in") for m in "qkv"]
        w13_in = [sem("w1_in"), sem("w3_in")]
        (const_in, w2_in, wo_in, gate_in, mhalf_set, wo_zero, stack_zero, k_zero, v_const, mem_zero, wqkv_hi_s, wqkv_lo_s, w13_hi_s, w1_lo_s, w3_lo_s,
         had_ps, had_sb, fly, w2_hi_s, w2_lo_s, gate_exp, gate_s) = [sem(n) for n in (
             "const_in w2_in wo_in gate_in mhalf_set wo_zero stack_zero k_zero v_const mem_zero wqkv_hi_s wqkv_lo_s w13_hi_s w1_lo_s w3_lo_s "
             "had_ps had_sb fly w2_hi_s w2_lo_s gate_exp gate_s").split()]
        (ln_stats, ln_mv, ln_ve, ln_rstd, ln_xn, hT_ps, hT_hi_s, hT_lo_s, h2T_ps, h2T_hi_s, h2T_lo_s) = [
            sem(n) for n in ("ln_stats ln_mv ln_ve ln_rstd ln_xn hT_ps hT_hi_s hT_lo_s h2T_ps h2T_hi_s h2T_lo_s").split()]
        (qk_ps, v_ps, v_sb, rope_prod, rope_sum, part_hi_s, part_lo_s, neg_s, elu_s, feat_s, kfT_ps,
         kfT_sb, mem_ps, mem_sb, lin_ps, lin_sb) = [sem(n) for n in (
             "qk_ps v_ps v_sb rope_prod rope_sum part_hi_s part_lo_s neg_s elu_s feat_s kfT_ps "
             "kfT_sb mem_ps mem_sb lin_ps lin_sb").split()]
        parts_out = [sem("parts_out0"), sem("parts_out1")]
        stack_in = [sem("stack_in0"), sem("stack_in1")]
        (score_ps, rowmax_s, maxT_ps, nm_hi_s, nm_lo_s, maxrow_in, exp_ps, prob_s, pv_group, att_sb, dencol_s,
         inv_s, ginv_s, rden_s, norm_att, norm_lin, comb_s, wo_ps, x2_s) = [sem(n) for n in (
             "score_ps rowmax_s maxT_ps nm_hi_s nm_lo_s maxrow_in exp_ps prob_s pv_group att_sb dencol_s "
             "inv_s ginv_s rden_s norm_att norm_lin comb_s wo_ps x2_s").split()]
        (up_ps, tanh_s, gated_s, hid_s, hid_hi_s, hid_lo_s, down_ps, y_s, y_out) = [sem(n) for n in (
            "up_ps tanh_s gated_s hid_s hid_hi_s hid_lo_s down_ps y_s y_out").split()]

        block = ctx.enter_context(nc.Block())
        ROUNDS = range(-1, NB + 1)
        def chunk(b, c):
            return FC * b + c if 0 <= b < NB else None

        def chunk_bank(n):
            return (exp_bank if n % FC in (7, 0, 1, 2) else score_bank)[n % 2]

        def has(b):
            return 0 <= b < NB

        PIECES = (slice(0, 2), slice(2, 3), slice(3, 4))
        NP = len(PIECES)

        LN_ORDER = []
        LN_ORDER.append((1, 0))
        for r in ROUNDS:
            if has(r - 1):
                LN_ORDER.append((2, r - 1))
            if has(r + 2):
                LN_ORDER.append((1, r + 2))
        LN = {key: n for n, key in enumerate(LN_ORDER)}

        def xn_read(n):
            which, b = LN_ORDER[n]
            return (hT_ps if which == 1 else h2T_ps), b + 1

        @block.sync
        def _(sp):
            def xv(ap, b):
                return ap[b].rearrange("(t p) d -> p t d", p=P)

            sp.dma_start(xs[:, 0], xv(x, 0)).then_inc(x_in[0], 16)
            for m, w in enumerate((wqT, wkT)):
                sp.dma_start(wqkv_raw[:, m], w.rearrange("(c p) n -> p c n", p=P)).then_inc(wqkv_in[m], 16)
            sp.dma_start(xs[:, 1], xv(x, 1)).then_inc(x_in[1], 16)
            for m, w in enumerate((w1T, w3T)):
                sp.dma_start(wide_raw[:, m], w.rearrange("(c p) n -> p c n", p=P)).then_inc(w13_in[m], 16)
            sp.wait_ge(wqkv_hi_s, 3)
            sp.wait_ge(wqkv_lo_s, 3)
            sp.dma_start(w2_raw, w2T.rearrange("(c p) n -> p c n", p=P)).then_inc(w2_in, 16)
            for b in range(2, NB):
                sp.dma_start(xs[:, b], xv(x, b)).then_inc(x_in[b], 16)
            sp.wait_ge(wo_zero, 1)
            for j in range(4):
                sp.dma_start(wo[STRIP * j:STRIP * j + HD, :, :],
                             woT.rearrange("(g j e) n -> j e g n", j=4, e=HD)[j]).then_inc(wo_in, 16)

            def write_parts(b, c):
                for half, (t, ready) in enumerate(((part_hi, part_hi_s), (part_lo, part_lo_s))):
                    sp.wait_ge(ready, DC * b + c + 1)
                    sp.dma_start(parts[b, half, c].rearrange("m p n -> p m n"), t[:, c].bitcast(F32)).then_inc(parts_out[c], 16)

            def load_stacks(b, c):
                sp.wait_ge(parts_out[c], 32 * (b + 1))
                if b == 0:
                    sp.wait_ge(stack_zero, 2)
                else:
                    sp.wait_ge(exp_ps, NH * (b - 1) + HH * (c + 1))
                for m, stack, slots in ((0, q_stack, (0, 1, 0)), (1, k_stack, (0, 0, 1))):
                    for s, half in enumerate(slots):
                        sp.dma_start(stack[HD * s:HD * s + HD, HH * c:HH * c + HH, :].bitcast(F32),
                                     parts[b, half, c, m].rearrange("(h d) n -> d h n", d=HD)).then_inc(stack_in[c], 16)

            def load_max(b):
                sp.wait_ge(nm_lo_s, b + 1)
                sp.dma_start(q_stack[MAXROW + 1:MAXROW + 2, :, :].rearrange("o h (t n) -> o (h t) n", t=TT).bitcast(F32),
                             nmT_lo[:].bitcast(F32)).then_inc(maxrow_in, 16)

            def store(b):
                sp.wait_ge(y_s, b + 1)
                sp.dma_start(xv(out, b), xs[:, b]).then_inc(y_out, 16)

            for r in ROUNDS:
                if has(r + 1):
                    for c in range(DC):
                        write_parts(r + 1, c)
                if has(r):
                    load_max(r)
                if has(r + 1):
                    for c in range(DC):
                        load_stacks(r + 1, c)
                if has(r - 2):
                    store(r - 2)
            store(NB - 1)
            sp.wait_ge(y_out, 16 * NB)
            for c in range(DC):
                sp.wait_ge(parts_out[c], 32 * NB)

        @block.scalar
        def _(act):
            act.dma_start(gcol[:], gate).then_inc(gate_in, 16)
            act.dma_start(cst[:], const).then_inc(const_in, 16)
            act.dma_start(wqkv_raw[:, 2], wvT.rearrange("(c p) n -> p c n", p=P)).then_inc(wqkv_in[2], 16)
            act.wait_ge(gate_in, 16)
            act.activation(gexp[:], gcol[:], ACT.Exp, scale=-1.0).then_inc(gate_exp, 1)
            for m in range(3):
                act.wait_ge(wqkv_in[m], 16)
                act.activation(wqkv_hi[:, m], wqkv_raw[:, m], ACT.Copy).then_inc(wqkv_hi_s, 1)

            def evac_hT(b):
                act.wait_ge(hT_ps, b + 1)
                if b >= 1:
                    act.wait_ge(v_ps, b)
                act.activation(hT_hi[:], misc_bank[0][:], ACT.Copy).then_inc(hT_hi_s, 1)

            def split_parts(b, c):
                act.wait_ge(rope_sum, DC * b + c + 1)
                if b >= 1:
                    act.wait_ge(parts_out[c], 32 * b)
                act.activation(part_hi[:, c], roped[:, c], ACT.Copy).then_inc(part_hi_s, 1)

            def evac_v(b):
                act.wait_ge(v_ps, b + 1)
                if b < 2:
                    act.wait_ge(v_const, 4)
                else:
                    act.wait_ge(pv_group, NG * (b - 1))
                act.activation(v_strips[b % 2][:, :, :, 0:HD],
                               misc_bank[0][:].rearrange("p t (h e) -> p t h e", e=HD), ACT.Copy).then_inc(v_sb, 1)

            def exp_elu(b):
                act.wait_ge(neg_s, b + 1)
                act.activation(elu, elu, ACT.Exp).then_inc(elu_s, 1)

            def evac_kfT(b):
                act.wait_ge(kfT_ps, b + 1)
                if b >= 1:
                    act.wait_ge(mem_ps, b)
                act.activation(kfT[:], misc_bank[0][:], ACT.Copy).then_inc(kfT_sb, 1)

            def evac_lin(b, u):
                act.wait_ge(lin_ps, 2 * b + u + 1)
                if b == 0:
                    act.wait_ge(w1_lo_s, 1)
                else:
                    act.wait_ge(comb_s, NP * b)
                act.activation(lin[:, 2 * u:2 * u + 2, :], misc_bank[u][:], ACT.Copy).then_inc(lin_sb, 1)

            def split_max(b):
                act.wait_ge(maxT_ps, b + 1)
                if b >= 1:
                    act.wait_ge(maxrow_in, 32 * b)
                act.activation(nmT_hi[:], pv_bank[0:TT * NH, 0, 0:P], ACT.Copy, scale=-1.0).then_inc(nm_hi_s, 1)
                act.wait_ge(nm_hi_s, b + 1)
                act.dma_start(q_stack[MAXROW:MAXROW + 1, :, :].rearrange("o h (t n) -> o (h t) n", t=TT).bitcast(F32),
                              nmT_hi[:].bitcast(F32)).then_inc(maxrow_in, 16)

            def exp_head(b, h):
                act.wait_ge(exp_ps, NH * b + h + 1)
                if NH * b + h >= 8:
                    act.wait_ge(pv_group, (NH * b + h - 8) // 4 + 1)
                act.activation(prob[:, h % 8], exp_bank[h % 2][:], ACT.Exp, scale=SCALE).then_inc(prob_s, 1)

            def evac_att(b, u):
                gs = PIECES[u]
                act.wait_ge(pv_group, NG * b + gs.stop)
                if b >= 1:
                    act.wait_ge(wo_ps, b)
                src = (pv_bank[:], pv_bank[:, 0:1], misc_bank[0][:, 0:1])[u]
                act.activation(att[:, gs, :], src, ACT.Copy).then_inc(att_sb, 1)

            def evac_h2T(b):
                act.wait_ge(h2T_ps, b + 1)
                if b >= 1:
                    act.wait_ge(up_ps, FC * b)
                act.activation(h2T_hi[:], pv_bank[:], ACT.Copy).then_inc(h2T_hi_s, 1)

            def ffn_tanh(n):
                act.wait_ge(up_ps, n + 1)
                if n == 0:
                    act.wait_ge(w1_lo_s, 1)
                if n >= 3:
                    act.wait_ge(hid_hi_s, n - 2)
                    act.wait_ge(hid_lo_s, n - 2)
                act.activation(ffn_work[n % 3], chunk_bank(n)[:, 0, :], ACT.Tanh, scale=0.5).then_inc(tanh_s, 1)

            def split_hid(n):
                act.wait_ge(hid_s, n + 1)
                if n >= 3:
                    act.wait_ge(down_ps, n - 2)
                act.activation(hid_hi[:, n % 3, :], ffn_work[n % 3], ACT.Copy).then_inc(hid_hi_s, 1)

            def ffn_step(n):
                if n is not None:
                    ffn_tanh(n)
                    if n % FC >= 1:
                        split_hid(n - 1)

            def split_wide(m):
                act.wait_ge(w13_in[m], 16)
                act.activation(w13_hi[:, m], wide_raw[:, m], ACT.Copy).then_inc(w13_hi_s, 1)

            def evac_hadamard(u):
                act.wait_ge(had_ps, u + 1)
                act.activation(w2_raw[:, 2 * u:2 * u + 2, :], exp_bank[u % 2][:], ACT.Copy, scale=1.0 / 64).then_inc(had_sb, 1)

            def split_w2():
                act.wait_ge(fly, 6)
                act.activation(w2_hi[:], w2_b, ACT.Copy).then_inc(w2_hi_s, 1)

            evac_hT(0)
            for m in range(2):
                split_wide(m)
            for r in ROUNDS:
                if has(r + 1):
                    split_parts(r + 1, 0)
                if has(r - 2):
                    ffn_tanh(chunk(r - 2, 7))
                if has(r + 1):
                    split_parts(r + 1, 1)
                if has(r - 2):
                    split_hid(chunk(r - 2, 7))
                if has(r - 1):
                    evac_h2T(r - 1)
                if has(r + 1):
                    evac_v(r + 1)
                if r < 0:
                    evac_hT(1)
                    evac_hadamard(0)
                    evac_hadamard(1)
                    exp_elu(0)
                    evac_hadamard(2)
                    evac_hadamard(3)
                    evac_kfT(0)
                    continue
                ffn_step(chunk(r - 1, 0))
                ffn_step(chunk(r - 1, 1))
                ffn_step(chunk(r - 1, 2))
                if has(r):
                    split_max(r)
                    evac_lin(r, 0)
                    evac_lin(r, 1)
                ffn_step(chunk(r - 1, 3))
                ffn_step(chunk(r - 1, 4))
                for g in range(NG):
                    if has(r):
                        exp_head(r, 4 * g)
                        exp_head(r, 4 * g + 1)
                    if g == 1 and has(r + 1):
                        exp_elu(r + 1)
                    if g == 2 and has(r + 2):
                        evac_hT(r + 2)
                    if g == 3:
                        if has(r):
                            evac_att(r, 0)
                        if has(r + 1):
                            evac_kfT(r + 1)
                    if g < 2 or (g == 2 and r == NB):
                        ffn_step(chunk(r - 1, 5 + g))
                    elif has(r - 1) and (g == 2 or r == NB):
                        split_hid(chunk(r - 1, 4 + g))
                    if has(r):
                        exp_head(r, 4 * g + 2)
                        exp_head(r, 4 * g + 3)
                if has(r):
                    evac_att(r, 1)
                    evac_att(r, 2)
                if r == 0:
                    split_w2()

        @block.gpsimd
        def _(pool):
            pool.memset(mhalf[:], -0.5).then_inc(mhalf_set, 1)
            pool.memset(q_stack[:].bitcast(F32), 0.0).then_inc(stack_zero, 1)

            def ln_power(n):
                if n == 0:
                    pool.wait_ge(mhalf_set, 1)
                pool.wait_ge(ln_ve, n + 1)
                if n >= 1:
                    pool.wait_ge(ln_xn, TT * n)
                pool.tensor_tensor(rstd[:], var_eps[:], mhalf[:], ALU.pow).then_inc(ln_rstd, 1)

            def rope_sums(b, c):
                pool.wait_ge(feat_s, b)
                pool.wait_ge(part_hi_s, DC * b)
                pool.wait_ge(part_lo_s, DC * b)
                pool.wait_ge(rope_prod, 4 * b + 2 * c + 2)
                pool.tensor_tensor(roped[:, c], prod[:, 2 * c], prod[:, 2 * c + 1],
                                   (ALU.subtract, ALU.add)[c]).then_inc(rope_sum, 1)

            def low_parts(b):
                for c in range(DC):
                    pool.wait_ge(part_hi_s, DC * b + c + 1)
                    pool.wait_ge(parts_out[c], 32 * b)
                    pool.tensor_tensor(part_lo[:, c], roped[:, c], part_hi[:, c].bitcast(F32), ALU.subtract).then_inc(part_lo_s, 1)

            def negative_part(b):
                pool.wait_ge(rope_sum, DC * (b + 1))
                pool.tensor_scalar(elu, roped[:], 0.0, None, ALU.min).then_inc(neg_s, 1)

            def hid_low(n):
                if n is None:
                    return
                pool.wait_ge(hid_hi_s, n + 1)
                if n >= 3:
                    pool.wait_ge(down_ps, n - 2)
                pool.tensor_tensor(hid_lo[:, n % 3, :], ffn_work[n % 3], hid_hi[:, n % 3, :].bitcast(F32),
                                   ALU.subtract).then_inc(hid_lo_s, 1)

            def norm_linear(b):
                pool.wait_ge(rden_s, (NP + 1) * b + 1)
                v = lin.rearrange("p g n -> p (g n)")
                pool.tensor_tensor(v, v, rden, ALU.mult).then_inc(norm_lin, 1)

            ln_power(0)
            pool.memset(k_stack[:].bitcast(F32), 0.0).then_inc(k_zero, 1)
            pool.wait_ge(k_zero, 1)
            pool.memset(k_stack[MAXROW:MAXROW + 2].bitcast(F32), 1.0).then_inc(stack_zero, 1)
            pool.wait_ge(stack_zero, 2)
            ln_power(1)
            pool.memset(wo[:], 0.0).then_inc(wo_zero, 1)
            pool.wait_ge(w13_hi_s, 2)
            pool.tensor_tensor(w13_lo[:, 1], wide_raw[:, 1], w13_hi[:, 1].bitcast(F32), ALU.subtract).then_inc(w3_lo_s, 1)
            for r in range(0, NB + 1):
                if has(r + 1):
                    rope_sums(r + 1, 0)
                if has(r - 1):
                    ln_power(LN[(2, r - 1)])
                if has(r + 1):
                    rope_sums(r + 1, 1)
                hid_low(chunk(r - 2, 7))
                if has(r + 1):
                    low_parts(r + 1)
                    negative_part(r + 1)
                hid_low(chunk(r - 1, 0))
                hid_low(chunk(r - 1, 1))
                for c in range(2, FC if r == NB else FC - 1):
                    hid_low(chunk(r - 1, c))
                    if c == 3 and has(r + 2):
                        ln_power(LN[(1, r + 2)])
                    if c == 5 and has(r):
                        norm_linear(r)
                if r == 0:
                    pool.wait_ge(w2_hi_s, 1)
                    pool.tensor_tensor(w2_lo[:], w2_b, w2_hi[:].bitcast(F32), ALU.subtract).then_inc(w2_lo_s, 1)

        @block.vector
        def _(dve):
            def zeros_and_ones():
                for k in range(2):
                    dve.memset(v_strips[k][:], 0.0).then_inc(v_const, 1)
                dve.memset(mem[:], 0.0).then_inc(mem_zero, 1)
                dve.wait_ge(v_const, 2)
                for k in range(2):
                    dve.memset(v_strips[k][:, :, :, HD:VW], 1.0).then_inc(v_const, 1)

            def ln_statistics(n):
                which, b = LN_ORDER[n]
                if which == 1:
                    dve.wait_ge(x_in[b], 16)
                else:
                    dve.wait_ge(x2_s, b + 1)
                if n >= 1:
                    dve.wait_ge(ln_mv, TT * n)
                for tt in range(TT):
                    dve.bn_stats(stats[:, tt, :], xs[:, b, tt, :]).then_inc(ln_stats, 1)
                if n >= 1:
                    dve.wait_ge(ln_xn, TT * n)
                for tt in range(TT):
                    dve.wait_ge(ln_stats, TT * n + tt + 1)
                    dve.bn_aggr(mv[:, tt, :], stats[:, tt, :]).then_inc(ln_mv, 1)
                dve.wait_ge(ln_mv, TT * (n + 1))
                if n >= 1:
                    dve.wait_ge(ln_rstd, n)
                dve.tensor_scalar(var_eps[:], mv[:, :, 1], EPS, None, ALU.add).then_inc(ln_ve, 1)

            def ln_normalise(n):
                which, b = LN_ORDER[n]
                dve.wait_ge(ln_rstd, n + 1)
                if n >= 1:
                    dve.wait_ge(*xn_read(n - 1))
                for tt in range(TT):
                    dve.tensor_scalar(xn[:, tt, :], xs[:, b, tt, :], mv[:, tt, 0:1], rstd[:, tt:tt + 1],
                                      ALU.subtract, ALU.mult).then_inc(ln_xn, 1)

            def low_hT(b):
                dve.wait_ge(hT_hi_s, b + 1)
                dve.tensor_tensor(hT_lo[:], misc_bank[0][:], hT_hi[:].bitcast(F32), ALU.subtract).then_inc(hT_lo_s, 1)

            def low_h2T(b):
                dve.wait_ge(h2T_hi_s, b + 1)
                dve.tensor_tensor(h2T_lo[:], pv_bank[:], h2T_hi[:].bitcast(F32), ALU.subtract).then_inc(h2T_lo_s, 1)

            def row_maxima(b, heads):
                for h in heads:
                    n = NH * b + h
                    dve.wait_ge(score_ps, n + 1)
                    if h == 0 and b >= 1:
                        dve.wait_ge(maxT_ps, b)
                    dve.tensor_reduce(rowmax[:, h, :], score_bank[h % 2][:], AX.X, ALU.max).then_inc(rowmax_s, 1)

            def rope_product(b, k):
                if b == 0:
                    dve.wait_ge(const_in, 16)
                else:
                    dve.wait_ge(rope_sum, 2 * b)
                    dve.wait_ge(feat_s, b)
                dve.wait_ge(qk_ps, 2 * (b + 1))
                c, table = ((0, cos2), (1, sin2), (1, cos2), (0, sin2))[k]
                dve.tensor_tensor(prod[:, k], misc_bank[c][:], table, ALU.mult).then_inc(rope_prod, 1)

            def first_rope_sums():
                for c, op in enumerate((ALU.subtract, ALU.add)):
                    dve.wait_ge(rope_prod, 2 * c + 2)
                    dve.tensor_tensor(roped[:, c], prod[:, 2 * c], prod[:, 2 * c + 1], op).then_inc(rope_sum, 1)

            def first_low_parts():
                for c in range(DC):
                    dve.wait_ge(part_hi_s, c + 1)
                    dve.tensor_tensor(part_lo[:, c], roped[:, c], part_hi[:, c].bitcast(F32), ALU.subtract).then_inc(part_lo_s, 1)

            def first_negative_part():
                dve.wait_ge(rope_sum, DC)
                dve.tensor_scalar(elu, roped[:], 0.0, None, ALU.min).then_inc(neg_s, 1)

            def features(b):
                dve.wait_ge(elu_s, b + 1)
                if b >= 1:
                    dve.wait_ge(lin_ps, 2 * b)
                dve.scalar_tensor_tensor(out=feat[:].rearrange("p c m n -> p (c m n)"),
                                         in0=roped[:].rearrange("p c m n -> p (c m n)"), scalar=1.0,
                                         in1=elu.rearrange("p c m n -> p (c m n)"),
                                         op0=ALU.add, op1=ALU.max).then_inc(feat_s, 1)

            def memory_strips(b):
                dve.wait_ge(mem_ps, b + 1)
                if b == 0:
                    dve.wait_ge(mem_zero, 1)
                else:
                    dve.wait_ge(lin_ps, 2 * b)
                for c in range(DC):
                    dve.tensor_tensor(mem[:, c, :, 0:VW],
                                      misc_bank[1][:, c, 0:HH * VW].rearrange("p (h e) -> p h e", e=VW),
                                      mask, ALU.mult).then_inc(mem_sb, 1)

            def weights(b, use):
                n = (NP + 1) * b + use
                groups = slice(0, NG) if use == 0 else PIECES[use - 1]
                cols = slice(groups.start * S, groups.stop * S)
                blocks = den_cols[:, cols].rearrange("p (k n) -> p k n", n=STRIP)
                if use == 0:
                    dve.wait_ge(lin_sb, 2 * (b + 1))
                    src = lin
                    if b == 0:
                        dve.wait_ge(gate_s, 3)
                        dve.wait_ge(fly, 6)
                        dve.wait_ge(had_ps, 4)
                    else:
                        dve.wait_ge(ginv_s, n)
                        dve.wait_ge(norm_att, NP * b)
                else:
                    dve.wait_ge(att_sb, NP * b + use)
                    src = att[:, groups, :]
                    dve.wait_ge(inv_s, n)
                dve.transpose(den_cols[:, cols], src.rearrange("p g n -> p (g n)")).then_inc(dencol_s, 1)
                dve.wait_ge(dencol_s, n + 1)
                if n >= 1:
                    dve.wait_ge(ginv_s, n)
                dve.reciprocal(inv[:, groups].rearrange("p g k -> p (g k)"), blocks[:, :, HD]).then_inc(inv_s, 1)
                dve.wait_ge(inv_s, n + 1)
                if n >= 1:
                    dve.wait_ge(rden_s, n)
                gw = gate2[:, 1 if use == 0 else 0, groups]
                width = [P, groups.stop - groups.start, S // STRIP]
                dve.tensor_tensor(ginv[:, groups], inv[:, groups], gw.unsqueeze(2).broadcast_to(width), ALU.mult).then_inc(ginv_s, 1)
                dve.wait_ge(ginv_s, n + 1)
                if use > 0:
                    dve.wait_ge(norm_lin, b + 1)
                full = [P, width[1] * width[2], STRIP]
                dve.transpose(rden[:, cols].rearrange("p (k n) -> p k n", n=STRIP),
                              ginv[:, groups].rearrange("p g k -> p (g k)").unsqueeze(2).broadcast_to(full)).then_inc(rden_s, 1)

            def combine(b, u):
                weights(b, u + 1)
                dve.wait_ge(rden_s, (NP + 1) * b + u + 2)
                gs = PIECES[u]
                piece = att[:, gs, :].rearrange("p g n -> p (g n)")
                dve.tensor_tensor(piece, piece, rden[:, gs.start * S:gs.stop * S], ALU.mult).then_inc(norm_att, 1)
                dve.wait_ge(norm_att, NP * b + u + 1)
                dve.wait_ge(norm_lin, b + 1)
                dve.tensor_tensor(piece, piece, lin[:, gs, :].rearrange("p g n -> p (g n)"), ALU.add).then_inc(comb_s, 1)

            def first_residual(b):
                dve.wait_ge(wo_ps, b + 1)
                dve.tensor_tensor(xs[:, b], xs[:, b], pv_bank[:], ALU.add).then_inc(x2_s, 1)

            def low_max(b):
                dve.wait_ge(nm_hi_s, b + 1)
                if b >= 1:
                    dve.wait_ge(maxrow_in, 32 * b)
                dve.scalar_tensor_tensor(out=nmT_lo[:], in0=pv_bank[0:TT * NH, 0, 0:P], scalar=-1.0,
                                         in1=nmT_hi[:].bitcast(F32), op0=ALU.mult, op1=ALU.subtract).then_inc(nm_lo_s, 1)

            def ffn_gate(n):
                if n is None:
                    return
                work = ffn_work[n % 3]
                dve.wait_ge(tanh_s, n + 1)
                dve.scalar_tensor_tensor(out=work, in0=work, scalar=1.0, in1=chunk_bank(n)[:, 0, :],
                                         op0=ALU.add, op1=ALU.mult).then_inc(gated_s, 1)
                dve.wait_ge(gated_s, n + 1)
                dve.tensor_tensor(work, work, chunk_bank(n)[:, 1, :], ALU.mult).then_inc(hid_s, 1)

            def second_residual(b):
                dve.wait_ge(down_ps, FC * (b + 1))
                dve.wait_ge(ln_xn, TT * (LN[(2, b)] + 1))
                dve.tensor_tensor(xs[:, b], xs[:, b], down_bank[:], ALU.add).then_inc(y_s, 1)

            def gate_weights():
                dve.wait_ge(gate_exp, 1)
                dve.tensor_scalar(gsum[:], gexp[:], 1.0, None, ALU.add).then_inc(gate_s, 1)
                dve.wait_ge(gate_s, 1)
                dve.reciprocal(gate2[:, 1], gsum[:]).then_inc(gate_s, 1)
                dve.wait_ge(gate_s, 2)
                dve.tensor_scalar(gate2[:, 0], gate2[:, 1], -1.0, 1.0, ALU.mult, ALU.add).then_inc(gate_s, 1)

            def butterfly(s):
                if s == 0:
                    dve.wait_ge(had_sb, 4)
                    dve.wait_ge(w3_lo_s, 1)
                else:
                    dve.wait_ge(fly, 2 * s)
                src, dst = ((w2_raw, w2_b), (w2_b, w2_raw), (w2_raw, w2_b))[s]
                i, o = (v.rearrange("p (o k i) n -> p o k (i n)", k=2, i=4 >> s) for v in (src, dst))
                for k, op in enumerate((ALU.add, ALU.subtract)):
                    dve.tensor_tensor(o[:, :, k], i[:, :, 0], i[:, :, 1], op).then_inc(fly, 1)

            zeros_and_ones()
            ln_statistics(0)
            ln_normalise(0)
            for m in range(3):
                dve.wait_ge(wqkv_hi_s, m + 1)
                dve.tensor_tensor(wqkv_lo[:, m], wqkv_raw[:, m], wqkv_hi[:, m].bitcast(F32), ALU.subtract).then_inc(wqkv_lo_s, 1)
                if m == 0:
                    low_hT(0)
            ln_statistics(1)
            for k in range(4):
                rope_product(0, k)
            first_rope_sums()
            ln_normalise(1)
            first_low_parts()
            first_negative_part()
            low_hT(1)
            dve.wait_ge(w13_hi_s, 1)
            dve.tensor_tensor(w13_lo[:, 0], wide_raw[:, 0], w13_hi[:, 0].bitcast(F32), ALU.subtract).then_inc(w1_lo_s, 1)
            gate_weights()
            features(0)
            butterfly(0)
            memory_strips(0)
            for r in range(0, NB + 1):
                for h in range(NH):
                    if has(r):
                        row_maxima(r, (h,))
                    if h == 13 and has(r - 2):
                        second_residual(r - 2)
                    if h == 1 and has(r - 1):
                        combine(r - 1, 2)
                    if 3 <= h < 7 and has(r + 1):
                        rope_product(r + 1, h - 3)
                    if h == 4 and has(r - 1):
                        first_residual(r - 1)
                        ln_statistics(LN[(2, r - 1)])
                    if h == 7:
                        ffn_gate(chunk(r - 2, 7))
                    if h == 5 and has(r - 1):
                        ln_normalise(LN[(2, r - 1)])
                    if h == 9 and has(r - 1):
                        low_h2T(r - 1)
                    if h in (12, 14):
                        ffn_gate(chunk(r - 1, h // 2 - 6))
                ffn_gate(chunk(r - 1, 2))
                if has(r):
                    low_max(r)
                    if r == 0:
                        butterfly(1)
                        butterfly(2)
                ffn_gate(chunk(r - 1, 3))
                if has(r):
                    weights(r, 0)
                if has(r + 2):
                    ln_statistics(LN[(1, r + 2)])
                ffn_gate(chunk(r - 1, 4))
                for g in range(NG):
                    if g == 0 and has(r + 2):
                        ln_normalise(LN[(1, r + 2)])
                    if g < 2 or (g == 2 and r == NB):
                        ffn_gate(chunk(r - 1, 5 + g))
                    if g == 1 and has(r + 1):
                        features(r + 1)
                    if g == 2 and has(r + 2):
                        low_hT(r + 2)
                    if g == 3 and has(r):
                        combine(r, 0)
                    if g == 3 and has(r + 1):
                        memory_strips(r + 1)
                if has(r):
                    combine(r, 1)
            second_residual(NB - 1)

        @block.tensor
        def _(pe):
            free = {}

            def claim(bank):
                if bank.name in free:
                    pe.wait_ge(*free[bank.name])
                return bank

            def three(out_ap, lhs, rhs, start, stop, **kw):
                pe.matmul(out_ap, lhs[0], rhs[0], start=start, stop=False, **kw)
                pe.matmul(out_ap, lhs[0], rhs[1], start=False, stop=False, **kw)
                return pe.matmul(out_ap, lhs[1], rhs[0], start=False, stop=stop, **kw)

            def transpose_rows(n):
                which, b = LN_ORDER[n]
                done, reader = ((hT_ps, hT_lo_s), (h2T_ps, h2T_lo_s))[which - 1]
                if n == 0:
                    pe.wait_ge(const_in, 16)
                pe.wait_ge(ln_xn, TT * (n + 1))
                bank = claim(misc_bank[0] if which == 1 else pv_bank)
                for c in range(DC):
                    for tt in range(TT):
                        mm = pe.transpose(bank[:, c, tt * P:tt * P + P], xn[:, tt, c * P:c * P + P], ident)
                mm.then_inc(done, 1)
                free[bank.name] = (reader, b + 1)

            def project_qk(b, part):
                if part == 0:
                    pe.wait_ge(hT_hi_s, b + 1)
                    pe.wait_ge(hT_lo_s, b + 1)
                if part < 2 and b == 0:
                    pe.wait_ge(wqkv_hi_s, part + 1)
                    pe.wait_ge(wqkv_lo_s, part + 1)
                c, m = divmod(part, 2)
                bank = claim(misc_bank[c]) if m == 0 else misc_bank[c]
                cols = slice(c * P, c * P + P)
                for k in range(DC):
                    mm = three(bank[:, m, :], (wqkv_hi[:, m, k, cols], wqkv_lo[:, m, k, cols]),
                               (hT_hi[:, k, :], hT_lo[:, k, :]), k == 0, k == DC - 1)
                if m == 1:
                    mm.then_inc(qk_ps, 1)
                free[bank.name] = (rope_prod, 4 * (b + 1))

            def project_v(b, tt):
                if b == 0:
                    pe.wait_ge(wqkv_hi_s, 3)
                    pe.wait_ge(wqkv_lo_s, 3)
                bank = claim(misc_bank[0]) if tt == 0 else misc_bank[0]
                rows = slice(tt * P, tt * P + P)
                for k in range(DC):
                    mm = three(bank[:, tt, :], (hT_hi[:, k, rows], hT_lo[:, k, rows]),
                               (wqkv_hi[:, 2, k, :], wqkv_lo[:, 2, k, :]), k == 0, k == DC - 1)
                if tt == TT - 1:
                    mm.then_inc(v_ps, 1)
                free[bank.name] = (v_sb, b + 1)

            def scores(b, heads):
                for h in heads:
                    if h % HH == 0:
                        pe.wait_ge(stack_in[h // HH], 96 * (b + 1))
                    bank = claim(score_bank[h % 2])
                    for tt in range(TT):
                        mm = pe.matmul(bank[:, tt, :], q_stack[0:MAXROW, h, tt * P:tt * P + P], k_stack[0:MAXROW, h, :],
                                       start=True, stop=True)
                    mm.then_inc(score_ps, 1)
                    free[bank.name] = (rowmax_s, NH * b + h + 1)

            def transpose_max(b):
                pe.wait_ge(rowmax_s, NH * (b + 1))
                bank = claim(pv_bank)
                pe.transpose(bank[0:TT * NH, 0, 0:P], rowmax[:].rearrange("p h t -> p (h t)"), ident).then_inc(maxT_ps, 1)
                free[bank.name] = (nm_lo_s, b + 1)

            def shifted_scores(b, h):
                if h == 0:
                    pe.wait_ge(maxrow_in, 32 * (b + 1))
                bank = claim(exp_bank[h % 2])
                for tt in range(TT):
                    mm = pe.matmul(bank[:, tt, :], k_stack[:, h, tt * P:tt * P + P], q_stack[:, h, :],
                                   start=True, stop=True)
                mm.then_inc(exp_ps, 1)
                free[bank.name] = (prob_s, NH * b + h + 1)

            def product_v(b, g):
                if g == 0:
                    pe.wait_ge(v_sb, b + 1)
                pe.wait_ge(prob_s, NH * b + 4 * g + 4)
                bank, half = (pv_bank, g % 2) if g < 3 else (misc_bank[0], 0)
                if g != 1:
                    claim(bank)
                for tt in range(TT):
                    for j in range(4):
                        h = 4 * g + j
                        mm = pe.matmul(bank[STRIP * j:STRIP * j + STRIP, half, :], v_strips[b % 2][:, tt, h, :],
                                       prob[:, h % 8, tt, :], start=(tt == 0), stop=(tt == TT - 1))
                mm.then_inc(pv_group, 1)
                free[bank.name] = (att_sb, NP * b + (1, 1, 2, 3)[g])

            def transpose_features(b):
                pe.wait_ge(feat_s, b + 1)
                bank = claim(misc_bank[0])
                for tt in range(TT):
                    for c in range(DC):
                        mm = pe.transpose(bank[:, tt, c * P:c * P + P], feat[:, c, 1, tt * P:tt * P + P], ident)
                mm.then_inc(kfT_ps, 1)
                free[bank.name] = (kfT_sb, b + 1)

            def memory(b):
                pe.wait_ge(kfT_sb, b + 1)
                pe.wait_ge(v_sb, b + 1)
                bank = claim(misc_bank[1])
                for c in range(DC):
                    for tt in range(TT):
                        mm = pe.matmul(bank[:, c, 0:HH * VW], kfT[:, tt, c * P:c * P + P],
                                       v_strips[b % 2][:, tt, HH * c:HH * c + HH, 0:VW],
                                       start=(tt == 0), stop=(tt == TT - 1))
                mm.then_inc(mem_ps, 1)
                free[bank.name] = (mem_sb, 2 * (b + 1))

            def read_memory(b, c):
                pe.wait_ge(mem_sb, 2 * (b + 1))
                bank = claim(misc_bank[c])
                for u in range(2):
                    mm = pe.matmul(bank[:, u, :], mem[:, c, 4 * u:4 * u + 4, :].rearrange("p h e -> p (h e)"),
                                   feat[:, c, 0, :], start=True, stop=True)
                mm.then_inc(lin_ps, 1)
                free[bank.name] = (lin_sb, 2 * b + c + 1)

            def project_out(b, g):
                if g == 0 and b == 0:
                    pe.wait_ge(wo_in, 64)
                pe.wait_ge(comb_s, NP * b + (1, 1, 2, 3)[g])
                bank = claim(pv_bank) if g == 0 else pv_bank
                for tt in range(TT):
                    mm = pe.matmul(bank[:, tt, :], att[:, g, tt * P:tt * P + P], wo[:, g, :],
                                   start=(g == 0 and tt == 0), stop=(g == NG - 1), skip_group_check=True)
                if g == NG - 1:
                    mm.then_inc(wo_ps, 1)
                free[bank.name] = (x2_s, b + 1)

            def ffn_up(n, m):
                if n is None:
                    return
                b, c = divmod(n, FC)
                if m == 0 and c == 0:
                    if b == 0:
                        pe.wait_ge(w13_hi_s, 2)
                        pe.wait_ge(w1_lo_s, 1)
                        pe.wait_ge(w3_lo_s, 1)
                    pe.wait_ge(h2T_hi_s, b + 1)
                    pe.wait_ge(h2T_lo_s, b + 1)
                bank = claim(chunk_bank(n)) if m == 0 else chunk_bank(n)
                cols = slice(c * P, c * P + P)
                for k in range(DC):
                    mm = three(bank[:, m, :], (w13_hi[:, m, k, cols], w13_lo[:, m, k, cols]),
                               (h2T_hi[:, k, :], h2T_lo[:, k, :]), k == 0, k == DC - 1)
                if m == 1:
                    mm.then_inc(up_ps, 1)
                free[bank.name] = (hid_s, n + 1)

            def ffn_down(n):
                if n is None:
                    return
                b, c = divmod(n, FC)
                if n == 0:
                    pe.wait_ge(w2_hi_s, 1)
                    pe.wait_ge(w2_lo_s, 1)
                pe.wait_ge(hid_hi_s, n + 1)
                pe.wait_ge(hid_lo_s, n + 1)
                bank = claim(down_bank) if c == 0 else down_bank
                for tt in range(TT):
                    rows = slice(tt * P, tt * P + P)
                    mm = three(bank[:, tt, :], (hid_hi[:, n % 3, rows], hid_lo[:, n % 3, rows]),
                               (w2_hi[:, c, :], w2_lo[:, c, :]), c == 0 and tt == 0, c == FC - 1,
                               skip_group_check=True)
                mm.then_inc(down_ps, 1)
                free[bank.name] = (y_s, b + 1)

            def hadamard(u):
                if u == 0:
                    pe.wait_ge(w2_in, 16)
                bank = claim(exp_bank[u % 2])
                for k in range(2):
                    mm = pe.matmul(bank[:, k, :], had, w2_raw[:, 2 * u + k, :], start=True, stop=True)
                mm.then_inc(had_ps, 1)
                free[bank.name] = (had_sb, u + 1)

            UP_AT = ((),) * 10 + ((0,), (1,), (2,), (3,), (4,), (5,))
            transpose_rows(0)
            for part in range(4):
                project_qk(0, part)
            for tt in range(TT):
                project_v(0, tt)
            transpose_rows(1)
            for u in range(4):
                hadamard(u)
            transpose_features(0)
            memory(0)
            for r in range(0, NB + 1):
                for h in range(NH):
                    if has(r):
                        scores(r, (h,))
                    if h < 4 and has(r + 1):
                        project_qk(r + 1, h)
                    if 1 <= h < 5 and has(r - 1):
                        project_out(r - 1, h - 1)
                    if h in (9, 10) and has(r + 1):
                        project_v(r + 1, h - 9)
                    if h == 8 and has(r - 1):
                        transpose_rows(LN[(2, r - 1)])
                    if h in (5, 6):
                        ffn_up(chunk(r - 2, 7), h - 5)
                    if h == 11:
                        ffn_down(chunk(r - 2, 7))
                    for i in UP_AT[h]:
                        ffn_up(chunk(r - 1, i // 2), i % 2)
                if has(r):
                    transpose_max(r)
                    read_memory(r, 0)
                ffn_down(chunk(r - 1, 0))
                if has(r):
                    read_memory(r, 1)
                for c in (3, 4):
                    for m in range(2):
                        ffn_up(chunk(r - 1, c), m)
                    ffn_down(chunk(r - 1, c - 2))
                for g in range(NG):
                    if has(r):
                        shifted_scores(r, 4 * g)
                    if g < 2 or (g == 2 and r == NB):
                        ffn_up(chunk(r - 1, 5 + g), 0)
                    if has(r):
                        shifted_scores(r, 4 * g + 1)
                    if g < 2 or (g == 2 and r == NB):
                        ffn_up(chunk(r - 1, 5 + g), 1)
                    if has(r):
                        shifted_scores(r, 4 * g + 2)
                    ffn_down(chunk(r - 1, 3 + g))
                    if has(r):
                        shifted_scores(r, 4 * g + 3)
                        if g >= 1:
                            product_v(r, g - 1)
                    if g == 1 and has(r + 2):
                        transpose_rows(LN[(1, r + 2)])
                    if g == 2 and has(r + 1):
                        transpose_features(r + 1)
                    if g == 3 and has(r + 1):
                        memory(r + 1)
                if has(r):
                    product_v(r, NG - 1)
            ffn_down(chunk(NB - 1, 7))


def kernel(L0_attn_hidden_states, L0_attn_Wq, L0_attn_Wk, L0_attn_Wv, L0_attn_Wo, L0_attn_gate,
           L0_ffn_W1, L0_ffn_W2, L0_ffn_W3):
    import concourse.bacc as bacc
    from concourse.bass_utils import run_bass_kernel_spmd

    def turned(w):
        return np.ascontiguousarray(np.asarray(w).T)

    gates = np.ascontiguousarray(np.repeat(np.asarray(L0_attn_gate).reshape(NG, 4).T, STRIP, axis=0))
    arrays = {
        "x": np.ascontiguousarray(L0_attn_hidden_states),
        "wqT": turned(L0_attn_Wq), "wkT": turned(L0_attn_Wk), "wvT": turned(L0_attn_Wv), "woT": turned(L0_attn_Wo),
        "gate": gates,
        "w1T": turned(L0_ffn_W1), "w3T": turned(L0_ffn_W3), "w2T": turned(L0_ffn_W2),
        "const": shape_constants(),
    }
    nc = bacc.Bacc("TRN2", target_bir_lowering=False, num_devices=1)
    aps = [nc.dram_tensor(f"in_{n}", a.shape, F32, kind="ExternalInput").ap() for n, a in arrays.items()]
    out = nc.dram_tensor("out_y", (NB, S, D), F32, kind="ExternalOutput").ap()
    build(nc, *aps, out)
    r = run_bass_kernel_spmd(nc, [{f"in_{n}": a for n, a in arrays.items()}], core_ids=[0])
    return r.results[0]["out_y"]
```

```python
from contextlib import ExitStack

import numpy as np

import concourse.bass as bass
from concourse import mybir

F32 = mybir.dt.float32
F32R = mybir.dt.float32r
ALU = mybir.AluOpType
ACT = mybir.ActivationFunctionType
AX = mybir.AxisListType

P = 128
NB, S, D = 4, 256, 256
NH, HD = 16, 16
FF = 1024
TT = S // P
DC = D // P
FC = FF // P
NG = NH // 4
HH = NH // DC
STRIP = 32
VW = HD + 1
MAXROW = 64
EPS = 1e-5
SCALE = HD ** -0.5
C_ID, C_HAD, C_COS, C_SIN, C_MASK = 0, P, 2 * P, 2 * P + S, 2 * P + 2 * S
NCONST = C_MASK + HH


def shape_constants():
    i = np.arange(P)
    bits = i[:, None] & i[None, :]
    parity = np.zeros_like(bits)
    for s in range(7):
        parity ^= (bits >> s) & 1
    inv_freq = (1.0 / np.float32(10000.0) ** (np.arange(0, D, 2, dtype=np.float32) / np.float32(D))).astype(np.float32)
    angle = inv_freq[:, None] * np.arange(S, dtype=np.float32)[None, :]
    c = np.zeros((P, NCONST), np.float32)
    c[:, C_ID:C_ID + P] = np.eye(P)
    c[:, C_HAD:C_HAD + P] = 1 - 2 * parity
    c[:, C_COS:C_COS + S] = np.cos(angle)
    c[:, C_SIN:C_SIN + S] = np.sin(angle)
    c[:, C_MASK:C_MASK + HH] = (i[:, None] // HD == np.arange(HH)[None, :])
    return c


def build(nc, x, wqT, wkT, wvT, woT, gate, w1T, w3T, w2T, const, out):
    with ExitStack() as ctx:
        def sb(name, shape, dt=F32):
            return ctx.enter_context(nc.sbuf_tensor(name, shape, dt))

        def sem(name):
            return ctx.enter_context(nc.semaphore(name))

        def bank(name):
            return ctx.enter_context(nc.psum_tensor(name, [P, 2, 256], F32))

        score_bank = [bank("score_bank0"), bank("score_bank1")]
        exp_bank = [bank("exp_bank0"), bank("exp_bank1")]
        pv_bank = bank("pv_bank")
        misc_bank = [bank("misc_bank0"), bank("misc_bank1")]
        qk_bank = misc_bank[::-1]
        down_bank = bank("down_bank")
        v_bank = (down_bank,) + (misc_bank[0],) * (NB - 1)

        xs = sb("xs", [P, NB, TT, D])
        cst = sb("cst", [P, NCONST])
        ident = cst[:, C_ID:C_ID + P]
        had = cst[:, C_HAD:C_HAD + P]
        cos2 = cst[:, C_COS:C_COS + S].unsqueeze(1).broadcast_to([P, 2, S])
        sin2 = cst[:, C_SIN:C_SIN + S].unsqueeze(1).broadcast_to([P, 2, S])
        mask = cst[:, C_MASK:C_MASK + HH].unsqueeze(2).broadcast_to([P, HH, VW])
        wide_raw = sb("wide_raw", [P, 2, DC, FF])
        narrow_raw = sb("narrow_raw", [P, 2048])
        wqkv_raw = narrow_raw[:, 0:3 * DC * D].rearrange("p (m c n) -> p m c n", m=3, c=DC)
        w2_raw = narrow_raw[:, :].rearrange("p (c n) -> p c n", c=FC)
        w2_b = wide_raw[:, 1, :, :].rearrange("p c (k n) -> p (c k) n", n=D)
        den_cols = narrow_raw[:, 0:NG * S]
        rden = narrow_raw[:, NG * S:]
        ffn_work = [wide_raw[:, 0, 0, 256 * k:256 * k + 256] for k in range(3)]
        wqkv_hi = sb("wqkv_hi", [P, 3, DC, D], F32R)
        wqkv_lo = sb("wqkv_lo", [P, 3, DC, D], F32R)
        w13_hi = sb("w13_hi", [P, 2, DC, FF], F32R)
        w13_lo = sb("w13_lo", [P, 2, DC, FF], F32R)
        w2_hi = sb("w2_hi", [P, FC, D], F32R)
        w2_lo = sb("w2_lo", [P, FC, D], F32R)
        wo = sb("wo", [P, NG, D])
        stats = sb("stats", [P, TT, 6])
        mv = sb("mv", [P, TT, 2])
        var_eps = sb("var_eps", [P, TT])
        rstd = sb("rstd", [P, TT])
        mhalf = sb("mhalf", [P, TT])
        xn = sb("xn", [P, TT, D])
        hT_hi = sb("hT_hi", [P, DC, S], F32R)
        hT_lo = sb("hT_lo", [P, DC, S], F32R)
        h2T_hi = sb("h2T_hi", [P, DC, S], F32R)
        h2T_lo = sb("h2T_lo", [P, DC, S], F32R)
        prod = sb("prod", [P, 4, 2, S])
        elu = prod[:, 0:2, :, :]
        roped = sb("roped", [P, DC, 2, S])
        part_hi = sb("part_hi", [P, DC, 2, S], F32R)
        part_lo = sb("part_lo", [P, DC, 2, S], F32R)
        feat = sb("feat", [P, DC, 2, S])
        q_stack = sb("q_stack", [P, NH, S], F32R)
        k_stack = sb("k_stack", [P, NH, S], F32R)
        v_strips = [sb("v_strips0", [P, TT, NH, STRIP]), sb("v_strips1", [P, TT, NH, STRIP])]
        kfT = sb("kfT", [P, TT, D])
        mem = sb("mem", [P, DC, HH, STRIP])
        rowmax = sb("rowmax", [P, NH, TT])
        nmT_hi = sb("nmT_hi", [TT * NH, P], F32R)
        nmT_lo = sb("nmT_lo", [TT * NH, P], F32R)
        prob = sb("prob", [P, 8, TT, S])
        att = sb("att", [P, NG, S])
        lin = wide_raw[:, 0, 1, :].rearrange("p (g n) -> p g n", g=NG)
        inv = sb("inv", [P, NG, S // STRIP])
        ginv = sb("ginv", [P, NG, S // STRIP])
        gcol = sb("gcol", [P, NG])
        gexp = sb("gexp", [P, NG])
        gsum = sb("gsum", [P, NG])
        gate2 = sb("gate2", [P, 2, NG])
        hid_hi = sb("hid_hi", [P, 3, S], F32R)
        hid_lo = sb("hid_lo", [P, 3, S], F32R)
        parts = nc.dram_tensor("parts", [NB, 2, DC, 2, P, S], F32, kind="Internal").ap()

        x_in = [sem(f"x_in{b}") for b in range(NB)]
        wqkv_in = [sem(f"w{m}_in") for m in "qkv"]
        w13_in = [sem("w1_in"), sem("w3_in")]
        (const_in, w2_in, wo_in, gate_in, mhalf_set, wo_zero, stack_zero, k_zero, v_const, mem_zero, wqkv_hi_s, wqkv_lo_s, w13_hi_s, w1_lo_s, w3_lo_s,
         had_ps, had_sb, fly, w2_hi_s, w2_lo_s, gate_exp, gate_s) = [sem(n) for n in (
             "const_in w2_in wo_in gate_in mhalf_set wo_zero stack_zero k_zero v_const mem_zero wqkv_hi_s wqkv_lo_s w13_hi_s w1_lo_s w3_lo_s "
             "had_ps had_sb fly w2_hi_s w2_lo_s gate_exp gate_s").split()]
        (ln_stats, ln_mv, ln_ve, ln_rstd, ln_xn, hT_ps, hT_hi_s, hT_lo_s, h2T_ps, h2T_hi_s, h2T_lo_s) = [
            sem(n) for n in ("ln_stats ln_mv ln_ve ln_rstd ln_xn hT_ps hT_hi_s hT_lo_s h2T_ps h2T_hi_s h2T_lo_s").split()]
        (qk_ps, v_ps, v_sb, rope_prod, rope_sum, part_hi_s, part_lo_s, neg_s, elu_s, feat_s, kfT_ps,
         kfT_sb, mem_ps, mem_sb, lin_ps, lin_sb) = [sem(n) for n in (
             "qk_ps v_ps v_sb rope_prod rope_sum part_hi_s part_lo_s neg_s elu_s feat_s kfT_ps "
             "kfT_sb mem_ps mem_sb lin_ps lin_sb").split()]
        parts_out = [sem("parts_out0"), sem("parts_out1")]
        stack_in = [sem("stack_in0"), sem("stack_in1")]
        (score_ps, rowmax_s, maxT_ps, nm_hi_s, nm_lo_s, maxrow_in, exp_ps, prob_s, pv_group, att_sb, dencol_s,
         inv_s, ginv_s, rden_s, norm_att, norm_lin, comb_s, wo_ps, x2_s) = [sem(n) for n in (
             "score_ps rowmax_s maxT_ps nm_hi_s nm_lo_s maxrow_in exp_ps prob_s pv_group att_sb dencol_s "
             "inv_s ginv_s rden_s norm_att norm_lin comb_s wo_ps x2_s").split()]
        (up_ps, tanh_s, gated_s, hid_s, hid_hi_s, hid_lo_s, down_ps, y_s, y_out) = [sem(n) for n in (
            "up_ps tanh_s gated_s hid_s hid_hi_s hid_lo_s down_ps y_s y_out").split()]

        block = ctx.enter_context(nc.Block())
        ROUNDS = range(-1, NB + 1)
        def chunk(b, c):
            return FC * b + c if 0 <= b < NB else None

        def chunk_bank(n):
            return (exp_bank if n % FC in (7, 0, 1, 2) else score_bank)[n % 2]

        def has(b):
            return 0 <= b < NB

        PIECES = (slice(0, 2), slice(2, 3), slice(3, 4))
        NP = len(PIECES)

        LN_ORDER = []
        LN_ORDER.append((1, 0))
        for r in ROUNDS:
            if has(r - 1):
                LN_ORDER.append((2, r - 1))
            if has(r + 2):
                LN_ORDER.append((1, r + 2))
        LN = {key: n for n, key in enumerate(LN_ORDER)}

        def xn_read(n):
            which, b = LN_ORDER[n]
            return (hT_ps if which == 1 else h2T_ps), b + 1

        def butterfly(engine, s):
            if s == 0:
                engine.wait_ge(had_sb, 4)
                engine.wait_ge(w3_lo_s, 1)
            else:
                engine.wait_ge(fly, 2 * s)
            src, dst = ((w2_raw, w2_b), (w2_b, w2_raw), (w2_raw, w2_b))[s]
            i, o = (v.rearrange("p (o k i) n -> p o k (i n)", k=2, i=4 >> s) for v in (src, dst))
            for k, op in enumerate((ALU.add, ALU.subtract)):
                engine.tensor_tensor(o[:, :, k], i[:, :, 0], i[:, :, 1], op).then_inc(fly, 1)

        @block.sync
        def _(sp):
            def xv(ap, b):
                return ap[b].rearrange("(t p) d -> p t d", p=P)

            sp.dma_start(xs[:, 0], xv(x, 0)).then_inc(x_in[0], 16)
            for m, w in enumerate((wqT, wkT)):
                sp.dma_start(wqkv_raw[:, m], w.rearrange("(c p) n -> p c n", p=P)).then_inc(wqkv_in[m], 16)
            sp.dma_start(xs[:, 1], xv(x, 1)).then_inc(x_in[1], 16)
            for m, w in enumerate((w1T, w3T)):
                sp.dma_start(wide_raw[:, m], w.rearrange("(c p) n -> p c n", p=P)).then_inc(w13_in[m], 16)
            sp.wait_ge(wqkv_hi_s, 3)
            sp.wait_ge(wqkv_lo_s, 3)
            sp.dma_start(w2_raw, w2T.rearrange("(c p) n -> p c n", p=P)).then_inc(w2_in, 16)
            for b in range(2, NB):
                sp.dma_start(xs[:, b], xv(x, b)).then_inc(x_in[b], 16)
            sp.wait_ge(wo_zero, 1)
            for j in range(4):
                sp.dma_start(wo[STRIP * j:STRIP * j + HD, :, :],
                             woT.rearrange("(g j e) n -> j e g n", j=4, e=HD)[j]).then_inc(wo_in, 16)

            def write_parts(b, c):
                for half, (t, ready) in enumerate(((part_hi, part_hi_s), (part_lo, part_lo_s))):
                    sp.wait_ge(ready, DC * b + c + 1)
                    sp.dma_start(parts[b, half, c].rearrange("m p n -> p m n"), t[:, c].bitcast(F32)).then_inc(parts_out[c], 16)

            def load_stacks(b, c):
                sp.wait_ge(parts_out[c], 32 * (b + 1))
                if b == 0:
                    sp.wait_ge(stack_zero, 2)
                else:
                    sp.wait_ge(exp_ps, NH * (b - 1) + HH * (c + 1))
                for m, stack, slots in ((0, q_stack, (0, 1, 0)), (1, k_stack, (0, 0, 1))):
                    for s, half in enumerate(slots):
                        sp.dma_start(stack[HD * s:HD * s + HD, HH * c:HH * c + HH, :].bitcast(F32),
                                     parts[b, half, c, m].rearrange("(h d) n -> d h n", d=HD)).then_inc(stack_in[c], 16)

            def load_max(b):
                sp.wait_ge(nm_lo_s, b + 1)
                sp.dma_start(q_stack[MAXROW + 1:MAXROW + 2, :, :].rearrange("o h (t n) -> o (h t) n", t=TT).bitcast(F32),
                             nmT_lo[:].bitcast(F32)).then_inc(maxrow_in, 16)

            def store(b):
                for tt in range(TT):
                    sp.wait_ge(y_s, TT * b + tt + 1)
                    sp.dma_start(out[b, tt * P:tt * P + P], xs[:, b, tt]).then_inc(y_out, 16)

            for r in ROUNDS:
                if has(r + 1):
                    for c in range(DC):
                        write_parts(r + 1, c)
                if has(r):
                    load_max(r)
                if has(r + 1):
                    for c in range(DC):
                        load_stacks(r + 1, c)
                if has(r - 2):
                    store(r - 2)
            store(NB - 1)
            sp.wait_ge(y_out, 16 * TT * NB)
            for c in range(DC):
                sp.wait_ge(parts_out[c], 32 * NB)

        @block.scalar
        def _(act):
            act.dma_start(gcol[:], gate).then_inc(gate_in, 16)
            act.dma_start(cst[:], const).then_inc(const_in, 16)
            act.dma_start(wqkv_raw[:, 2], wvT.rearrange("(c p) n -> p c n", p=P)).then_inc(wqkv_in[2], 16)
            act.wait_ge(gate_in, 16)
            act.activation(gexp[:], gcol[:], ACT.Exp, scale=-1.0).then_inc(gate_exp, 1)
            for m in range(3):
                act.wait_ge(wqkv_in[m], 16)
                act.activation(wqkv_hi[:, m], wqkv_raw[:, m], ACT.Copy).then_inc(wqkv_hi_s, 1)

            def evac_hT(b):
                act.wait_ge(hT_ps, b + 1)
                if b >= 1:
                    act.wait_ge(v_ps, b)
                act.activation(hT_hi[:], misc_bank[0][:], ACT.Copy).then_inc(hT_hi_s, 1)

            def split_parts(b, c):
                act.wait_ge(rope_sum, DC * b + c + 1)
                if b >= 1:
                    act.wait_ge(parts_out[c], 32 * b)
                act.activation(part_hi[:, c], roped[:, c], ACT.Copy).then_inc(part_hi_s, 1)

            def evac_v(b):
                act.wait_ge(v_ps, b + 1)
                if b < 2:
                    act.wait_ge(v_const, 4)
                else:
                    act.wait_ge(pv_group, NG * (b - 1))
                act.activation(v_strips[b % 2][:, :, :, 0:HD],
                               v_bank[b][:].rearrange("p t (h e) -> p t h e", e=HD), ACT.Copy).then_inc(v_sb, 1)

            def exp_elu(b):
                act.wait_ge(neg_s, b + 1)
                act.activation(elu, elu, ACT.Exp).then_inc(elu_s, 1)

            def evac_kfT(b):
                act.wait_ge(kfT_ps, b + 1)
                if b >= 1:
                    act.wait_ge(mem_ps, b)
                act.activation(kfT[:], misc_bank[0][:], ACT.Copy).then_inc(kfT_sb, 1)

            def evac_lin(b, u):
                act.wait_ge(lin_ps, 2 * b + u + 1)
                if b == 0:
                    act.wait_ge(w1_lo_s, 1)
                else:
                    act.wait_ge(comb_s, NP * b)
                act.activation(lin[:, 2 * u:2 * u + 2, :], misc_bank[u][:], ACT.Copy).then_inc(lin_sb, 1)

            def split_max(b):
                act.wait_ge(maxT_ps, b + 1)
                if b >= 1:
                    act.wait_ge(maxrow_in, 32 * b)
                act.activation(nmT_hi[:], pv_bank[0:TT * NH, 0, 0:P], ACT.Copy, scale=-1.0).then_inc(nm_hi_s, 1)
                act.wait_ge(nm_hi_s, b + 1)
                act.dma_start(q_stack[MAXROW:MAXROW + 1, :, :].rearrange("o h (t n) -> o (h t) n", t=TT).bitcast(F32),
                              nmT_hi[:].bitcast(F32)).then_inc(maxrow_in, 16)

            def exp_head(b, h):
                act.wait_ge(exp_ps, NH * b + h + 1)
                if NH * b + h >= 8:
                    act.wait_ge(pv_group, (NH * b + h - 8) // 4 + 1)
                act.activation(prob[:, h % 8], exp_bank[h % 2][:], ACT.Exp, scale=SCALE).then_inc(prob_s, 1)

            def evac_att(b, u):
                gs = PIECES[u]
                act.wait_ge(pv_group, NG * b + gs.stop)
                if b >= 1:
                    act.wait_ge(wo_ps, b)
                src = (pv_bank[:], pv_bank[:, 0:1], misc_bank[1][:, 0:1])[u]
                act.activation(att[:, gs, :], src, ACT.Copy).then_inc(att_sb, 1)

            def evac_x2(b):
                act.wait_ge(ln_stats, TT * (LN[(2, b)] + 1))
                act.activation(xs[:, b], pv_bank[:], ACT.Copy).then_inc(x2_s, 1)

            def evac_h2T(b):
                act.wait_ge(h2T_ps, b + 1)
                if b >= 1:
                    act.wait_ge(up_ps, FC * b)
                act.activation(h2T_hi[:], pv_bank[:], ACT.Copy).then_inc(h2T_hi_s, 1)

            def ffn_tanh(n):
                act.wait_ge(up_ps, n + 1)
                if n == 0:
                    act.wait_ge(w1_lo_s, 1)
                if n >= 3:
                    act.wait_ge(hid_hi_s, n - 2)
                    act.wait_ge(hid_lo_s, n - 2)
                act.activation(ffn_work[n % 3], chunk_bank(n)[:, 0, :], ACT.Tanh, scale=0.5).then_inc(tanh_s, 1)

            def split_hid(n):
                act.wait_ge(hid_s, n + 1)
                if n >= 3:
                    act.wait_ge(down_ps, n - 2)
                act.activation(hid_hi[:, n % 3, :], ffn_work[n % 3], ACT.Copy).then_inc(hid_hi_s, 1)

            def ffn_step(n):
                if n is not None:
                    ffn_tanh(n)
                    if n % FC >= 1:
                        split_hid(n - 1)

            def split_wide(m):
                act.wait_ge(w13_in[m], 16)
                act.activation(w13_hi[:, m], wide_raw[:, m], ACT.Copy).then_inc(w13_hi_s, 1)

            def evac_hadamard(u):
                act.wait_ge(had_ps, u + 1)
                act.activation(w2_raw[:, 2 * u:2 * u + 2, :], exp_bank[u % 2][:], ACT.Copy, scale=1.0 / 64).then_inc(had_sb, 1)

            def split_w2():
                act.wait_ge(fly, 6)
                act.activation(w2_hi[:], w2_b, ACT.Copy).then_inc(w2_hi_s, 1)

            evac_hT(0)
            for m in range(2):
                split_wide(m)
            for r in ROUNDS:
                if has(r - 1):
                    evac_x2(r - 1)
                if r < 0:
                    evac_v(0)
                if has(r + 1):
                    split_parts(r + 1, 0)
                if r == 0:
                    evac_hadamard(2)
                    evac_hadamard(3)
                if has(r - 2):
                    ffn_tanh(chunk(r - 2, 7))
                if has(r + 1):
                    split_parts(r + 1, 1)
                if has(r - 2):
                    split_hid(chunk(r - 2, 7))
                if has(r - 1):
                    evac_h2T(r - 1)
                if r >= 0 and has(r + 1):
                    evac_v(r + 1)
                if r < 0:
                    exp_elu(0)
                    evac_hT(1)
                    evac_hadamard(0)
                    evac_kfT(0)
                    evac_hadamard(1)
                    continue
                ffn_step(chunk(r - 1, 0))
                ffn_step(chunk(r - 1, 1))
                if has(r):
                    split_max(r)
                ffn_step(chunk(r - 1, 2))
                if has(r):
                    evac_lin(r, 0)
                    evac_lin(r, 1)
                ffn_step(chunk(r - 1, 3))
                for h in range(NH):
                    if has(r):
                        exp_head(r, h)
                    if h in (2, 6, 12):
                        ffn_step(chunk(r - 1, {2: 4, 6: 5, 12: 6}[h]))
                    if h == 5 and has(r + 1):
                        exp_elu(r + 1)
                    if h == 8 and has(r + 2):
                        evac_hT(r + 2)
                    if h == 11 and has(r):
                        evac_att(r, 0)
                    if h == 15 and has(r - 1):
                        if r == NB:
                            ffn_tanh(chunk(r - 1, 7))
                        split_hid(chunk(r - 1, 6))
                if has(r):
                    evac_att(r, 1)
                if has(r + 1):
                    evac_kfT(r + 1)
                if has(r):
                    evac_att(r, 2)
                if r == 0:
                    split_w2()
            split_hid(chunk(NB - 1, 7))

        @block.gpsimd
        def _(pool):
            pool.memset(mhalf[:], -0.5).then_inc(mhalf_set, 1)
            pool.memset(q_stack[:].bitcast(F32), 0.0).then_inc(stack_zero, 1)

            def ln_power(n):
                if n == 0:
                    pool.wait_ge(mhalf_set, 1)
                pool.wait_ge(ln_ve, n + 1)
                if n >= 1:
                    pool.wait_ge(ln_xn, TT * n)
                pool.tensor_tensor(rstd[:], var_eps[:], mhalf[:], ALU.pow).then_inc(ln_rstd, 1)

            def rope_sums(b, c):
                pool.wait_ge(feat_s, b)
                pool.wait_ge(part_hi_s, DC * b)
                pool.wait_ge(part_lo_s, DC * b)
                pool.wait_ge(rope_prod, 4 * b + 2 * c + 2)
                pool.tensor_tensor(roped[:, c], prod[:, 2 * c], prod[:, 2 * c + 1],
                                   (ALU.subtract, ALU.add)[c]).then_inc(rope_sum, 1)

            def low_parts(b):
                for c in range(DC):
                    pool.wait_ge(part_hi_s, DC * b + c + 1)
                    pool.wait_ge(parts_out[c], 32 * b)
                    pool.tensor_tensor(part_lo[:, c], roped[:, c], part_hi[:, c].bitcast(F32), ALU.subtract).then_inc(part_lo_s, 1)

            def negative_part(b):
                pool.wait_ge(rope_sum, DC * (b + 1))
                pool.tensor_scalar(elu, roped[:], 0.0, None, ALU.min).then_inc(neg_s, 1)

            def hid_low(n):
                if n is None:
                    return
                pool.wait_ge(hid_hi_s, n + 1)
                if n >= 3:
                    pool.wait_ge(down_ps, n - 2)
                pool.tensor_tensor(hid_lo[:, n % 3, :], ffn_work[n % 3], hid_hi[:, n % 3, :].bitcast(F32),
                                   ALU.subtract).then_inc(hid_lo_s, 1)

            def norm_linear(b):
                pool.wait_ge(rden_s, (NP + 1) * b + 1)
                v = lin.rearrange("p g n -> p (g n)")
                pool.tensor_tensor(v, v, rden, ALU.mult).then_inc(norm_lin, 1)

            ln_power(0)
            pool.memset(k_stack[:].bitcast(F32), 0.0).then_inc(k_zero, 1)
            pool.wait_ge(k_zero, 1)
            pool.memset(k_stack[MAXROW:MAXROW + 2].bitcast(F32), 1.0).then_inc(stack_zero, 1)
            pool.wait_ge(stack_zero, 2)
            ln_power(1)
            pool.memset(wo[:], 0.0).then_inc(wo_zero, 1)
            for m, done in enumerate((w1_lo_s, w3_lo_s)):
                pool.wait_ge(w13_hi_s, m + 1)
                pool.tensor_tensor(w13_lo[:, m], wide_raw[:, m], w13_hi[:, m].bitcast(F32), ALU.subtract).then_inc(done, 1)
            for r in range(0, NB + 1):
                if has(r + 1):
                    rope_sums(r + 1, 0)
                if has(r - 1):
                    ln_power(LN[(2, r - 1)])
                if has(r + 1):
                    rope_sums(r + 1, 1)
                hid_low(chunk(r - 2, 7))
                if has(r + 1):
                    low_parts(r + 1)
                if r == 0:
                    butterfly(pool, 0)
                if has(r + 1):
                    negative_part(r + 1)
                hid_low(chunk(r - 1, 0))
                hid_low(chunk(r - 1, 1))
                for c in range(2, FC if r == NB else FC - 1):
                    hid_low(chunk(r - 1, c))
                    if c == 3 and has(r + 2):
                        ln_power(LN[(1, r + 2)])
                    if c == 4 and has(r):
                        norm_linear(r)
                if r == 0:
                    pool.wait_ge(w2_hi_s, 1)
                    pool.tensor_tensor(w2_lo[:], w2_b, w2_hi[:].bitcast(F32), ALU.subtract).then_inc(w2_lo_s, 1)

        @block.vector
        def _(dve):
            def zeros_and_ones():
                for k in range(2):
                    dve.memset(v_strips[k][:], 0.0).then_inc(v_const, 1)
                dve.memset(mem[:], 0.0).then_inc(mem_zero, 1)
                dve.wait_ge(v_const, 2)
                for k in range(2):
                    dve.memset(v_strips[k][:, :, :, HD:VW], 1.0).then_inc(v_const, 1)

            def ln_statistics(n):
                which, b = LN_ORDER[n]
                if which == 1:
                    dve.wait_ge(x_in[b], 16)
                else:
                    dve.wait_ge(wo_ps, b + 1)
                src = xs[:, b] if which == 1 else pv_bank
                if n >= 1:
                    dve.wait_ge(ln_mv, TT * n)
                for tt in range(TT):
                    dve.bn_stats(stats[:, tt, :], src[:, tt, :]).then_inc(ln_stats, 1)
                if n >= 1:
                    dve.wait_ge(ln_xn, TT * n)
                for tt in range(TT):
                    dve.wait_ge(ln_stats, TT * n + tt + 1)
                    dve.bn_aggr(mv[:, tt, :], stats[:, tt, :]).then_inc(ln_mv, 1)
                dve.wait_ge(ln_mv, TT * (n + 1))
                if n >= 1:
                    dve.wait_ge(ln_rstd, n)
                dve.tensor_scalar(var_eps[:], mv[:, :, 1], EPS, None, ALU.add).then_inc(ln_ve, 1)

            def ln_normalise(n):
                which, b = LN_ORDER[n]
                if which == 2:
                    dve.wait_ge(x2_s, b + 1)
                dve.wait_ge(ln_rstd, n + 1)
                if n >= 1:
                    dve.wait_ge(*xn_read(n - 1))
                for tt in range(TT):
                    dve.tensor_scalar(xn[:, tt, :], xs[:, b, tt, :], mv[:, tt, 0:1], rstd[:, tt:tt + 1],
                                      ALU.subtract, ALU.mult).then_inc(ln_xn, 1)

            def low_hT(b):
                dve.wait_ge(hT_hi_s, b + 1)
                dve.tensor_tensor(hT_lo[:], misc_bank[0][:], hT_hi[:].bitcast(F32), ALU.subtract).then_inc(hT_lo_s, 1)

            def low_h2T(b):
                dve.wait_ge(h2T_hi_s, b + 1)
                dve.tensor_tensor(h2T_lo[:], pv_bank[:], h2T_hi[:].bitcast(F32), ALU.subtract).then_inc(h2T_lo_s, 1)

            def row_maxima(b, heads):
                for h in heads:
                    n = NH * b + h
                    dve.wait_ge(score_ps, n + 1)
                    if h == 0 and b >= 1:
                        dve.wait_ge(maxT_ps, b)
                    dve.tensor_reduce(rowmax[:, h, :], score_bank[h % 2][:], AX.X, ALU.max).then_inc(rowmax_s, 1)

            def rope_product(b, k):
                if b == 0:
                    dve.wait_ge(const_in, 16)
                else:
                    dve.wait_ge(rope_sum, 2 * b)
                    dve.wait_ge(feat_s, b)
                dve.wait_ge(qk_ps, 2 * (b + 1))
                c, table = ((0, cos2), (1, sin2), (1, cos2), (0, sin2))[k]
                dve.tensor_tensor(prod[:, k], qk_bank[c][:], table, ALU.mult).then_inc(rope_prod, 1)

            def first_rope_sum(c):
                dve.wait_ge(rope_prod, 2 * c + 2)
                dve.tensor_tensor(roped[:, c], prod[:, 2 * c], prod[:, 2 * c + 1],
                                  (ALU.subtract, ALU.add)[c]).then_inc(rope_sum, 1)

            def first_low_part(c):
                dve.wait_ge(part_hi_s, c + 1)
                dve.tensor_tensor(part_lo[:, c], roped[:, c], part_hi[:, c].bitcast(F32), ALU.subtract).then_inc(part_lo_s, 1)

            def first_negative_part():
                dve.wait_ge(rope_sum, DC)
                dve.tensor_scalar(elu, roped[:], 0.0, None, ALU.min).then_inc(neg_s, 1)

            def features(b):
                dve.wait_ge(elu_s, b + 1)
                if b >= 1:
                    dve.wait_ge(lin_ps, 2 * b)
                dve.scalar_tensor_tensor(out=feat[:].rearrange("p c m n -> p (c m n)"),
                                         in0=roped[:].rearrange("p c m n -> p (c m n)"), scalar=1.0,
                                         in1=elu.rearrange("p c m n -> p (c m n)"),
                                         op0=ALU.add, op1=ALU.max).then_inc(feat_s, 1)

            def memory_strips(b):
                dve.wait_ge(mem_ps, b + 1)
                if b == 0:
                    dve.wait_ge(mem_zero, 1)
                else:
                    dve.wait_ge(lin_ps, 2 * b)
                for c in range(DC):
                    dve.tensor_tensor(mem[:, c, :, 0:VW],
                                      misc_bank[0][:, c, 0:HH * VW].rearrange("p (h e) -> p h e", e=VW),
                                      mask, ALU.mult).then_inc(mem_sb, 1)

            def weights(b, use):
                n = (NP + 1) * b + use
                groups = slice(0, NG) if use == 0 else PIECES[use - 1]
                cols = slice(groups.start * S, groups.stop * S)
                blocks = den_cols[:, cols].rearrange("p (k n) -> p k n", n=STRIP)
                if use == 0:
                    dve.wait_ge(lin_sb, 2 * (b + 1))
                    src = lin
                    if b == 0:
                        dve.wait_ge(gate_s, 3)
                        dve.wait_ge(fly, 6)
                        dve.wait_ge(had_ps, 4)
                    else:
                        dve.wait_ge(ginv_s, n)
                        dve.wait_ge(norm_att, NP * b)
                else:
                    dve.wait_ge(att_sb, NP * b + use)
                    src = att[:, groups, :]
                    dve.wait_ge(inv_s, n)
                dve.transpose(den_cols[:, cols], src.rearrange("p g n -> p (g n)")).then_inc(dencol_s, 1)
                dve.wait_ge(dencol_s, n + 1)
                if n >= 1:
                    dve.wait_ge(ginv_s, n)
                dve.reciprocal(inv[:, groups].rearrange("p g k -> p (g k)"), blocks[:, :, HD]).then_inc(inv_s, 1)
                dve.wait_ge(inv_s, n + 1)
                if n >= 1:
                    dve.wait_ge(rden_s, n)
                gw = gate2[:, 1 if use == 0 else 0, groups]
                width = [P, groups.stop - groups.start, S // STRIP]
                dve.tensor_tensor(ginv[:, groups], inv[:, groups], gw.unsqueeze(2).broadcast_to(width), ALU.mult).then_inc(ginv_s, 1)
                dve.wait_ge(ginv_s, n + 1)
                if use > 0:
                    dve.wait_ge(norm_lin, b + 1)
                full = [P, width[1] * width[2], STRIP]
                dve.transpose(rden[:, cols].rearrange("p (k n) -> p k n", n=STRIP),
                              ginv[:, groups].rearrange("p g k -> p (g k)").unsqueeze(2).broadcast_to(full)).then_inc(rden_s, 1)

            def combine(b, u):
                weights(b, u + 1)
                dve.wait_ge(rden_s, (NP + 1) * b + u + 2)
                gs = PIECES[u]
                piece = att[:, gs, :].rearrange("p g n -> p (g n)")
                dve.tensor_tensor(piece, piece, rden[:, gs.start * S:gs.stop * S], ALU.mult).then_inc(norm_att, 1)
                dve.wait_ge(norm_att, NP * b + u + 1)
                dve.wait_ge(norm_lin, b + 1)
                dve.tensor_tensor(piece, piece, lin[:, gs, :].rearrange("p g n -> p (g n)"), ALU.add).then_inc(comb_s, 1)

            def low_max(b):
                dve.wait_ge(nm_hi_s, b + 1)
                if b >= 1:
                    dve.wait_ge(maxrow_in, 32 * b)
                dve.scalar_tensor_tensor(out=nmT_lo[:], in0=pv_bank[0:TT * NH, 0, 0:P], scalar=-1.0,
                                         in1=nmT_hi[:].bitcast(F32), op0=ALU.mult, op1=ALU.subtract).then_inc(nm_lo_s, 1)

            def ffn_gate(n):
                if n is None:
                    return
                work = ffn_work[n % 3]
                dve.wait_ge(tanh_s, n + 1)
                dve.scalar_tensor_tensor(out=work, in0=work, scalar=1.0, in1=chunk_bank(n)[:, 0, :],
                                         op0=ALU.add, op1=ALU.mult).then_inc(gated_s, 1)
                dve.wait_ge(gated_s, n + 1)
                dve.tensor_tensor(work, work, chunk_bank(n)[:, 1, :], ALU.mult).then_inc(hid_s, 1)

            def second_residual(b):
                dve.wait_ge(down_ps, FC * (b + 1))
                dve.wait_ge(x2_s, b + 1)
                for tt in range(TT):
                    dve.tensor_tensor(xs[:, b, tt], xs[:, b, tt], down_bank[:, tt], ALU.add).then_inc(y_s, 1)

            def gate_weights():
                dve.wait_ge(gate_exp, 1)
                dve.tensor_scalar(gsum[:], gexp[:], 1.0, None, ALU.add).then_inc(gate_s, 1)
                dve.wait_ge(gate_s, 1)
                dve.reciprocal(gate2[:, 1], gsum[:]).then_inc(gate_s, 1)
                dve.wait_ge(gate_s, 2)
                dve.tensor_scalar(gate2[:, 0], gate2[:, 1], -1.0, 1.0, ALU.mult, ALU.add).then_inc(gate_s, 1)

            zeros_and_ones()
            ln_statistics(0)
            ln_normalise(0)
            for m in range(3):
                dve.wait_ge(wqkv_hi_s, m + 1)
                dve.tensor_tensor(wqkv_lo[:, m], wqkv_raw[:, m], wqkv_hi[:, m].bitcast(F32), ALU.subtract).then_inc(wqkv_lo_s, 1)
                if m == 0:
                    low_hT(0)
            ln_statistics(1)
            rope_product(0, 0)
            rope_product(0, 1)
            first_rope_sum(0)
            rope_product(0, 2)
            first_low_part(0)
            rope_product(0, 3)
            first_rope_sum(1)
            first_low_part(1)
            ln_normalise(1)
            first_negative_part()
            features(0)
            low_hT(1)
            gate_weights()
            row_maxima(0, (0, 1))
            memory_strips(0)
            for r in range(0, NB + 1):
                for h in range(NH):
                    if has(r) and h >= 2:
                        row_maxima(r, (h,))
                    if h == 2 and has(r - 1):
                        combine(r - 1, 2)
                    if 3 <= h < 7 and has(r + 1):
                        rope_product(r + 1, h - 3)
                    if h == 4 and has(r - 1):
                        ln_statistics(LN[(2, r - 1)])
                    if h == 7:
                        ffn_gate(chunk(r - 2, 7))
                    if h == 5 and has(r - 1):
                        ln_normalise(LN[(2, r - 1)])
                    if h == 9 and has(r - 1):
                        low_h2T(r - 1)
                    if h == 12:
                        ffn_gate(chunk(r - 1, 0))
                if has(r):
                    low_max(r)
                ffn_gate(chunk(r - 1, 1))
                ffn_gate(chunk(r - 1, 2))
                if has(r - 2):
                    second_residual(r - 2)
                if has(r + 2):
                    ln_statistics(LN[(1, r + 2)])
                ffn_gate(chunk(r - 1, 3))
                if r == 0:
                    butterfly(dve, 1)
                if has(r + 2):
                    ln_normalise(LN[(1, r + 2)])
                if r == 0:
                    butterfly(dve, 2)
                ffn_gate(chunk(r - 1, 4))
                if has(r):
                    weights(r, 0)
                if has(r + 1):
                    features(r + 1)
                ffn_gate(chunk(r - 1, 5))
                if has(r + 2):
                    low_hT(r + 2)
                ffn_gate(chunk(r - 1, 6))
                if has(r):
                    combine(r, 0)
                if has(r + 1):
                    row_maxima(r + 1, (0,))
                if has(r):
                    combine(r, 1)
                if has(r + 1):
                    row_maxima(r + 1, (1,))
                    memory_strips(r + 1)
            ffn_gate(chunk(NB - 1, 7))
            second_residual(NB - 1)

        @block.tensor
        def _(pe):
            free = {}

            def claim(bank):
                if bank.name in free:
                    pe.wait_ge(*free[bank.name])
                return bank

            def three(out_ap, lhs, rhs, start, stop, **kw):
                pe.matmul(out_ap, lhs[0], rhs[0], start=start, stop=False, **kw)
                pe.matmul(out_ap, lhs[0], rhs[1], start=False, stop=False, **kw)
                return pe.matmul(out_ap, lhs[1], rhs[0], start=False, stop=stop, **kw)

            def transpose_rows(n):
                which, b = LN_ORDER[n]
                done, reader = ((hT_ps, hT_lo_s), (h2T_ps, h2T_lo_s))[which - 1]
                if n == 0:
                    pe.wait_ge(const_in, 16)
                pe.wait_ge(ln_xn, TT * (n + 1))
                bank = claim(misc_bank[0] if which == 1 else pv_bank)
                for c in range(DC):
                    for tt in range(TT):
                        mm = pe.transpose(bank[:, c, tt * P:tt * P + P], xn[:, tt, c * P:c * P + P], ident)
                mm.then_inc(done, 1)
                free[bank.name] = (reader, b + 1)

            def project_qk(b, part):
                if part == 0:
                    pe.wait_ge(hT_hi_s, b + 1)
                    pe.wait_ge(hT_lo_s, b + 1)
                if part < 2 and b == 0:
                    pe.wait_ge(wqkv_hi_s, part + 1)
                    pe.wait_ge(wqkv_lo_s, part + 1)
                c, m = divmod(part, 2)
                bank = claim(qk_bank[c]) if m == 0 else qk_bank[c]
                cols = slice(c * P, c * P + P)
                for k in range(DC):
                    mm = three(bank[:, m, :], (wqkv_hi[:, m, k, cols], wqkv_lo[:, m, k, cols]),
                               (hT_hi[:, k, :], hT_lo[:, k, :]), k == 0, k == DC - 1)
                if m == 1:
                    mm.then_inc(qk_ps, 1)
                free[bank.name] = (rope_prod, 4 * (b + 1))

            def project_v(b, tt):
                if b == 0:
                    pe.wait_ge(wqkv_hi_s, 3)
                    pe.wait_ge(wqkv_lo_s, 3)
                bank = claim(v_bank[b]) if tt == 0 else v_bank[b]
                rows = slice(tt * P, tt * P + P)
                for k in range(DC):
                    mm = three(bank[:, tt, :], (hT_hi[:, k, rows], hT_lo[:, k, rows]),
                               (wqkv_hi[:, 2, k, :], wqkv_lo[:, 2, k, :]), k == 0, k == DC - 1)
                if tt == TT - 1:
                    mm.then_inc(v_ps, 1)
                free[bank.name] = (v_sb, b + 1)

            def scores(b, heads):
                for h in heads:
                    if h % HH == 0:
                        pe.wait_ge(stack_in[h // HH], 96 * (b + 1))
                    bank = claim(score_bank[h % 2])
                    for tt in range(TT):
                        mm = pe.matmul(bank[:, tt, :], q_stack[0:MAXROW, h, tt * P:tt * P + P], k_stack[0:MAXROW, h, :],
                                       start=True, stop=True)
                    mm.then_inc(score_ps, 1)
                    free[bank.name] = (rowmax_s, NH * b + h + 1)

            def transpose_max(b):
                pe.wait_ge(rowmax_s, NH * (b + 1))
                bank = claim(pv_bank)
                pe.transpose(bank[0:TT * NH, 0, 0:P], rowmax[:].rearrange("p h t -> p (h t)"), ident).then_inc(maxT_ps, 1)
                free[bank.name] = (nm_lo_s, b + 1)

            def shifted_scores(b, h):
                if h == 0:
                    pe.wait_ge(maxrow_in, 32 * (b + 1))
                bank = claim(exp_bank[h % 2])
                for tt in range(TT):
                    mm = pe.matmul(bank[:, tt, :], k_stack[:, h, tt * P:tt * P + P], q_stack[:, h, :],
                                   start=True, stop=True)
                mm.then_inc(exp_ps, 1)
                free[bank.name] = (prob_s, NH * b + h + 1)

            def product_v(b, g, tt):
                if g == 0 and tt == 0:
                    pe.wait_ge(v_sb, b + 1)
                bank, half = (pv_bank, g % 2) if g < 3 else (misc_bank[1], 0)
                if tt == 0:
                    pe.wait_ge(prob_s, NH * b + 4 * g + 4)
                    if g != 1:
                        claim(bank)
                for j in range(4):
                    h = 4 * g + j
                    mm = pe.matmul(bank[STRIP * j:STRIP * j + STRIP, half, :], v_strips[b % 2][:, tt, h, :],
                                   prob[:, h % 8, tt, :], start=(tt == 0), stop=(tt == TT - 1))
                if tt == TT - 1:
                    mm.then_inc(pv_group, 1)
                free[bank.name] = (att_sb, NP * b + (1, 1, 2, 3)[g])

            def transpose_features(b):
                pe.wait_ge(feat_s, b + 1)
                bank = claim(misc_bank[0])
                for tt in range(TT):
                    for c in range(DC):
                        mm = pe.transpose(bank[:, tt, c * P:c * P + P], feat[:, c, 1, tt * P:tt * P + P], ident)
                mm.then_inc(kfT_ps, 1)
                free[bank.name] = (kfT_sb, b + 1)

            def memory(b):
                pe.wait_ge(kfT_sb, b + 1)
                pe.wait_ge(v_sb, b + 1)
                bank = claim(misc_bank[0])
                for c in range(DC):
                    for tt in range(TT):
                        mm = pe.matmul(bank[:, c, 0:HH * VW], kfT[:, tt, c * P:c * P + P],
                                       v_strips[b % 2][:, tt, HH * c:HH * c + HH, 0:VW],
                                       start=(tt == 0), stop=(tt == TT - 1))
                mm.then_inc(mem_ps, 1)
                free[bank.name] = (mem_sb, 2 * (b + 1))

            def read_memory(b, c):
                pe.wait_ge(mem_sb, 2 * (b + 1))
                bank = claim(misc_bank[c])
                for u in range(2):
                    mm = pe.matmul(bank[:, u, :], mem[:, c, 4 * u:4 * u + 4, :].rearrange("p h e -> p (h e)"),
                                   feat[:, c, 0, :], start=True, stop=True)
                mm.then_inc(lin_ps, 1)
                free[bank.name] = (lin_sb, 2 * b + c + 1)

            def residual_in(b):
                bank = claim(pv_bank)
                for tt in range(TT):
                    pe.matmul(bank[:, tt, :], ident, xs[:, b, tt, :], start=(tt == 0), stop=False, skip_group_check=True)

            def project_out(b, g):
                if g == 0 and b == 0:
                    pe.wait_ge(wo_in, 64)
                pe.wait_ge(comb_s, NP * b + (1, 1, 2, 3)[g])
                bank = pv_bank
                for tt in range(TT):
                    mm = pe.matmul(bank[:, tt, :], att[:, g, tt * P:tt * P + P], wo[:, g, :],
                                   start=False, stop=(g == NG - 1), skip_group_check=True)
                if g == NG - 1:
                    mm.then_inc(wo_ps, 1)
                free[bank.name] = (x2_s, b + 1)

            def ffn_up(n, m):
                if n is None:
                    return
                b, c = divmod(n, FC)
                if m == 0 and c == 0:
                    if b == 0:
                        pe.wait_ge(w13_hi_s, 2)
                        pe.wait_ge(w1_lo_s, 1)
                        pe.wait_ge(w3_lo_s, 1)
                    pe.wait_ge(h2T_hi_s, b + 1)
                bank = claim(chunk_bank(n)) if m == 0 else chunk_bank(n)
                cols = slice(c * P, c * P + P)
                for k in range(DC):
                    for w in (w13_hi, w13_lo):
                        pe.matmul(bank[:, m, :], w[:, m, k, cols], h2T_hi[:, k, :], start=(k == 0 and w is w13_hi), stop=False)
                if m == 0 and c == 0:
                    pe.wait_ge(h2T_lo_s, b + 1)
                for k in range(DC):
                    mm = pe.matmul(bank[:, m, :], w13_hi[:, m, k, cols], h2T_lo[:, k, :], start=False, stop=(k == DC - 1))
                if m == 1:
                    mm.then_inc(up_ps, 1)
                free[bank.name] = (hid_s, n + 1)

            def ffn_down(n):
                if n is None:
                    return
                b, c = divmod(n, FC)
                if n == 0:
                    pe.wait_ge(w2_hi_s, 1)
                    pe.wait_ge(w2_lo_s, 1)
                pe.wait_ge(hid_hi_s, n + 1)
                bank = claim(down_bank) if c == 0 else down_bank
                for tt in range(TT):
                    for w in (w2_hi, w2_lo):
                        pe.matmul(bank[:, tt, :], hid_hi[:, n % 3, tt * P:tt * P + P], w[:, c, :],
                                  start=(c == 0 and tt == 0 and w is w2_hi), stop=False, skip_group_check=True)
                pe.wait_ge(hid_lo_s, n + 1)
                for tt in range(TT):
                    mm = pe.matmul(bank[:, tt, :], hid_lo[:, n % 3, tt * P:tt * P + P], w2_hi[:, c, :],
                                   start=False, stop=(c == FC - 1), skip_group_check=True)
                mm.then_inc(down_ps, 1)
                free[bank.name] = (y_s, TT * (b + 1))

            def hadamard(u):
                if u == 0:
                    pe.wait_ge(w2_in, 16)
                bank = claim(exp_bank[u % 2])
                for k in range(2):
                    mm = pe.matmul(bank[:, k, :], had, w2_raw[:, 2 * u + k, :], start=True, stop=True)
                mm.then_inc(had_ps, 1)
                free[bank.name] = (had_sb, u + 1)

            UP_AT = ((),) * 10 + ((0,), (1,), (2,), (3,), (4,), (5,))
            UP_IN_EXP = {0: (4, 0), 1: (4, 1), 3: (5, 0), 4: (5, 1), 8: (6, 0), 11: (6, 1)}
            DOWN_IN_EXP = {2: 2, 7: 3, 12: 4}
            transpose_rows(0)
            for part in range(4):
                project_qk(0, part)
            for tt in range(TT):
                project_v(0, tt)
            transpose_rows(1)
            hadamard(0)
            transpose_features(0)
            hadamard(1)
            scores(0, (0, 1))
            memory(0)
            for r in range(0, NB + 1):
                for h in range(NH):
                    if has(r) and h >= 2:
                        scores(r, (h,))
                    if h < 4 and has(r + 1):
                        project_qk(r + 1, h)
                    if h in (6, 7) and r == 0:
                        hadamard(h - 4)
                    if h == 0 and has(r - 1):
                        residual_in(r - 1)
                    if 1 <= h < 5 and has(r - 1):
                        project_out(r - 1, h - 1)
                    if h in (9, 10) and has(r + 1):
                        project_v(r + 1, h - 9)
                    if h == 8 and has(r - 1):
                        transpose_rows(LN[(2, r - 1)])
                    if h in (6, 7):
                        ffn_up(chunk(r - 2, 7), h - 6)
                    if h == 10:
                        ffn_down(chunk(r - 2, 7))
                    for i in UP_AT[h]:
                        ffn_up(chunk(r - 1, i // 2), i % 2)
                if has(r):
                    transpose_max(r)
                    read_memory(r, 0)
                    read_memory(r, 1)
                for m in range(2):
                    ffn_up(chunk(r - 1, 3), m)
                ffn_down(chunk(r - 1, 0))
                ffn_down(chunk(r - 1, 1))
                for h in range(NH):
                    if has(r):
                        shifted_scores(r, h)
                    if h in UP_IN_EXP:
                        c, m = UP_IN_EXP[h]
                        ffn_up(chunk(r - 1, c), m)
                    if has(r) and h >= 5 and h % 4 in (1, 2):
                        product_v(r, h // 4 - 1, h % 4 - 1)
                    if h == 7 and has(r + 2):
                        transpose_rows(LN[(1, r + 2)])
                    if h in DOWN_IN_EXP:
                        ffn_down(chunk(r - 1, DOWN_IN_EXP[h]))
                if r == NB:
                    for m in range(2):
                        ffn_up(chunk(r - 1, 7), m)
                if has(r + 1):
                    transpose_features(r + 1)
                ffn_down(chunk(r - 1, 5))
                if has(r + 1):
                    scores(r + 1, (0, 1))
                if has(r):
                    for tt in range(TT):
                        product_v(r, NG - 1, tt)
                if has(r + 1):
                    memory(r + 1)
                ffn_down(chunk(r - 1, 6))
            ffn_down(chunk(NB - 1, 7))


def kernel(L0_attn_hidden_states, L0_attn_Wq, L0_attn_Wk, L0_attn_Wv, L0_attn_Wo, L0_attn_gate,
           L0_ffn_W1, L0_ffn_W2, L0_ffn_W3):
    import concourse.bacc as bacc
    from concourse.bass_utils import run_bass_kernel_spmd

    def turned(w):
        return np.ascontiguousarray(np.asarray(w).T)

    gates = np.ascontiguousarray(np.repeat(np.asarray(L0_attn_gate).reshape(NG, 4).T, STRIP, axis=0))
    arrays = {
        "x": np.ascontiguousarray(L0_attn_hidden_states),
        "wqT": turned(L0_attn_Wq), "wkT": turned(L0_attn_Wk), "wvT": turned(L0_attn_Wv), "woT": turned(L0_attn_Wo),
        "gate": gates,
        "w1T": turned(L0_ffn_W1), "w3T": turned(L0_ffn_W3), "w2T": turned(L0_ffn_W2),
        "const": shape_constants(),
    }
    nc = bacc.Bacc("TRN2", target_bir_lowering=False, num_devices=1)
    aps = [nc.dram_tensor(f"in_{n}", a.shape, F32, kind="ExternalInput").ap() for n, a in arrays.items()]
    out = nc.dram_tensor("out_y", (NB, S, D), F32, kind="ExternalOutput").ap()
    build(nc, *aps, out)
    r = run_bass_kernel_spmd(nc, [{f"in_{n}": a for n, a in arrays.items()}], core_ids=[0])
    return r.results[0]["out_y"]
```
